# Optimizing a Trainium2 kernel written in Bass

```python
import numpy as np
import jax
import jax.numpy as jnp

def _softmax(x, axis=-1):
    return jax.nn.softmax(x, axis=axis)

def _gelu(x):
    return jax.nn.gelu(x, approximate=True)

def _silu(x):
    return jax.nn.silu(x)

def _sigmoid(x):
    return jax.nn.sigmoid(x)

def _layernorm(x, axis=-1, eps=1e-05):
    m = jnp.mean(x, axis=axis, keepdims=True)
    v = jnp.var(x, axis=axis, keepdims=True)
    return (x - m) / jnp.sqrt(v + eps)

def _scatter_add(tgt, idx, src, axis=0):
    return tgt.at[idx].add(src)

def _segment_sum(src, seg, n):
    return jax.ops.segment_sum(src, seg, n)
kernel_name = 'mk_seq_preln_d1_jaxref_r4_da95c1'

def setup_inputs(seed: int=0):
    np.random.seed(seed)
    _w = jnp.asarray

    def _L0_attn_setup():
        import jax, jax.numpy as jnp
        import numpy as np
        B, S, D = (4, 512, 256)
        key = jax.random.key(seed)
        k1, k2, k3, k4 = jax.random.split(key, 4)
        x = jax.random.normal(k1, (B, S, D), dtype=jnp.float32)
        Qw = jax.random.normal(k2, (D, D), dtype=jnp.float32) / 40
        Kw = jax.random.normal(k3, (D, D), dtype=jnp.float32) / 40
        Vw = jax.random.normal(k4, (D, D), dtype=jnp.float32) / 40
        return {'x': x, 'Qw': Qw, 'Kw': Kw, 'Vw': Vw}
    _L0_attn_in = _L0_attn_setup()

    def _L0_ffn_setup():
        import jax, jax.numpy as jnp
        import numpy as np
        D_IN, D_H, D_OUT = (256, 256, 256)
        D_MOE = 1024
        N_EXPERTS = 8
        TOP_K = 2
        key = jax.random.key(seed)
        ks = jax.random.split(key, 10)
        s = lambda d: 1.0 / np.sqrt(d)
        x = jax.random.normal(ks[0], (2, 512, D_IN), dtype=jnp.float32)
        W_in = jax.random.normal(ks[1], (D_IN, D_H), dtype=jnp.float32) * s(D_IN)
        b_in = jnp.zeros((D_H,), jnp.float32)
        W_gate = jax.random.normal(ks[2], (D_H, N_EXPERTS), dtype=jnp.float32) * s(D_H)
        b_gate = jnp.zeros((N_EXPERTS,), jnp.float32)
        W1 = jax.random.normal(ks[3], (N_EXPERTS, D_H, D_MOE), dtype=jnp.float32) * s(D_H)
        b1 = jnp.zeros((N_EXPERTS, D_MOE), jnp.float32)
        W2 = jax.random.normal(ks[4], (N_EXPERTS, D_MOE, D_H), dtype=jnp.float32) * s(D_MOE)
        b2 = jnp.zeros((N_EXPERTS, D_H), jnp.float32)
        W_out = jax.random.normal(ks[5], (D_H, D_OUT), dtype=jnp.float32) * s(D_H)
        b_out = jnp.zeros((D_OUT,), jnp.float32)
        return {'x': x, 'W_in': W_in, 'b_in': b_in, 'W_gate': W_gate, 'b_gate': b_gate, 'W1': W1, 'b1': b1, 'W2': W2, 'b2': b2, 'W_out': W_out, 'b_out': b_out}
    _L0_ffn_in = _L0_ffn_setup()
    _d = {'L0_attn_x': _L0_attn_in['x'], 'L0_attn_Qw': _L0_attn_in['Qw'], 'L0_attn_Kw': _L0_attn_in['Kw'], 'L0_attn_Vw': _L0_attn_in['Vw'], 'L0_ffn_W_in': _L0_ffn_in['W_in'], 'L0_ffn_b_in': _L0_ffn_in['b_in'], 'L0_ffn_W_gate': _L0_ffn_in['W_gate'], 'L0_ffn_b_gate': _L0_ffn_in['b_gate'], 'L0_ffn_W1': _L0_ffn_in['W1'], 'L0_ffn_b1': _L0_ffn_in['b1'], 'L0_ffn_W2': _L0_ffn_in['W2'], 'L0_ffn_b2': _L0_ffn_in['b2'], 'L0_ffn_W_out': _L0_ffn_in['W_out'], 'L0_ffn_b_out': _L0_ffn_in['b_out']}
    _x0 = _d['L0_attn_x']
    _d['L0_attn_x'] = jax.random.normal(jax.random.fold_in(jax.random.key(seed), 1), (1, 4096, 256), dtype=_x0.dtype)
    del _x0
    return _d

def reference(L0_attn_x, L0_attn_Qw, L0_attn_Kw, L0_attn_Vw, L0_ffn_W_in, L0_ffn_b_in, L0_ffn_W_gate, L0_ffn_b_gate, L0_ffn_W1, L0_ffn_b1, L0_ffn_W2, L0_ffn_b2, L0_ffn_W_out, L0_ffn_b_out):

    def _L0_attn_ref(x, Qw, Kw, Vw):
        import jax, jax.numpy as jnp
        import numpy as np
        B, S, D = (4, 512, 256)
        Q = x @ Qw
        K = x @ Kw
        V = x @ Vw
        d = x.shape[-1]
        S_len = x.shape[-2]
        mask = jnp.where(jnp.tril(jnp.ones((S_len, S_len), dtype=x.dtype)) == 0, -jnp.inf, 0.0).astype(x.dtype)
        scores = jnp.einsum('bqd,bkd->bqk', Q, K) / jnp.sqrt(jnp.asarray(d, x.dtype))
        scores = scores + mask
        attn = jax.nn.softmax(scores, axis=-1)
        return jnp.einsum('bqk,bkd->bqd', attn, V)

    def _L0_ffn_ref(x, W_in, b_in, W_gate, b_gate, W1, b1, W2, b2, W_out, b_out):
        import jax, jax.numpy as jnp
        import numpy as np
        D_IN, D_H, D_OUT = (256, 256, 256)
        D_MOE = 1024
        N_EXPERTS = 8
        TOP_K = 2
        B, S, _ = x.shape
        h = x @ W_in + b_in
        t = h.reshape(B * S, -1)
        logits = t @ W_gate + b_gate
        probs = jax.nn.softmax(logits, axis=-1)
        topv, topi = jax.lax.top_k(probs, TOP_K)
        topv = topv / jnp.sum(topv, axis=-1, keepdims=True)
        route = jnp.zeros_like(probs).at[jnp.arange(t.shape[0])[:, None], topi].set(topv)
        mid = jax.nn.relu(jnp.einsum('nd,edh->neh', t, W1) + b1)
        eout = jnp.einsum('neh,ehd->ned', mid, W2) + b2
        moe_out = jnp.einsum('ne,ned->nd', route, eout)
        out = moe_out.reshape(B, S, -1) @ W_out + b_out
        return out
    x = L0_attn_x
    x = x + _L0_attn_ref(_layernorm(x, axis=-1), L0_attn_Qw, L0_attn_Kw, L0_attn_Vw)
    x = x + _L0_ffn_ref(_layernorm(x, axis=-1), L0_ffn_W_in, L0_ffn_b_in, L0_ffn_W_gate, L0_ffn_b_gate, L0_ffn_W1, L0_ffn_b1, L0_ffn_W2, L0_ffn_b2, L0_ffn_W_out, L0_ffn_b_out)
    return x

_drawn_inputs = setup_inputs


def setup_inputs(seed=0):
    import zlib

    import numpy as np

    out = dict(_drawn_inputs(seed))
    spreads = {'L0_ffn_b_in': (0.0, 0.1),
     'L0_ffn_b_gate': (0.0, 0.1),
     'L0_ffn_b1': (0.0, 0.1),
     'L0_ffn_b2': (0.0, 0.1),
     'L0_ffn_b_out': (0.0, 0.1)}
    factors = {}
    for name, (base, spread) in spreads.items():
        noise = np.random.default_rng([zlib.crc32(name.encode()), seed]).standard_normal(out[name].shape)
        drawn = base * np.exp(spread * noise) if base else spread * noise
        out[name] = jnp.asarray(drawn.astype(out[name].dtype))
    for name, factor in factors.items():
        out[name] = (out[name] * factor).astype(out[name].dtype)
    return out
```

```python
from contextlib import ExitStack

import concourse.bass as bass
from concourse import mybir

F32 = mybir.dt.float32
F32R = mybir.dt.float32r
BF16 = mybir.dt.bfloat16
I32 = mybir.dt.int32
U32 = mybir.dt.uint32
ALU = mybir.AluOpType
ACT = mybir.ActivationFunctionType
AX = mybir.AxisListType

P = 128
EPS = 1e-5
NEG = -3.0e38
RSQRT_SEED = 0x5F3759DF


def rows_bcast(dram, n):
    return dram.rearrange("(a n) -> a n", a=1).partition_broadcast(n).rearrange("p a n -> p (a n)")


def mm3(pe, out, w, m, start, stop):
    pe.matmul(out, w[0], m[0], start=start, stop=False)
    pe.matmul(out, w[0], m[1], start=False, stop=False)
    return pe.matmul(out, w[1], m[0], start=False, stop=stop)


def make_plan(NT):
    NH = NT // 2
    nc_of = lambda i: i // 4 + 1
    plan = [("wT", 0), ("wT", 1), ("wT", 2), ("M", 0), ("G", 0), ("ln1", 0), ("xT", 0), ("qm", 0),
            ("v", 0), ("ln1", 1)]
    for s in range(NT + 7):
        new = [("qk", s, c) for c in range(nc_of(s))] if s < NT else []
        if 1 <= s <= NT:
            plan += [("mx", s - 1)] + [("ex", s - 1, c) for c in range(min(2, nc_of(s - 1)))]
        if new:
            plan.append(new.pop(0))
        if 2 <= s <= NT + 1:
            plan.append(("fin", s - 2))
        if s % 2 == 1 and s >= 3 and (s - 3) // 2 < NH:
            plan.append(("ln2", (s - 3) // 2))
        if 1 <= s <= NT:
            n = nc_of(s - 1)
            for c in range(n):
                if new:
                    plan.append(new.pop(0))
                plan.append(("tp", s - 1, c))
                if c + 2 < n:
                    plan.append(("ex", s - 1, c + 2))
                if c >= 1:
                    plan.append(("pv", s - 1, c - 1))
            plan += new
            plan.append(("pv", s - 1, n - 1))
        else:
            plan += new
        k = s // 2 + 1
        if s % 2 == 0:
            if k < NH:
                plan.append(("xT", k))
            if k + 1 < NH:
                plan.append(("ln1", k + 1))
            if 0 <= (s - 4) // 2 < NH:
                plan += [("t", (s - 4) // 2, 0), ("t", (s - 4) // 2, 1), ("route", (s - 4) // 2)]
        else:
            if k < NH:
                plan += [("qm", k), ("v", k)]
            if 0 <= (s - 3) // 2 < NH:
                plan.append(("fT", (s - 3) // 2))
            if 0 <= (s - 5) // 2 < NH:
                plan.append(("pre", (s - 5) // 2))
    return plan


def build_kernel(nc, x_in, Qw, Kw, Vw, W_in, b_in, W_gate, b_gate, W1, b1, W2, b2, W_out, b_out, out):
    S, D = x_in.shape[1], x_in.shape[2]
    E, F = W1.shape[0], W1.shape[2]
    K2 = 2
    NT = S // P
    NH = NT // 2
    DC = D // P
    CH = 4 * P
    NCH = S // CH
    HC = F // P
    TS = 2 * P
    REGION = S + TS
    NTILES = (K2 * S + E * (TS - 1)) // TS
    ROW = D + 1
    NOWHERE = 1.0e6
    SCALE = 1.0 / float(D) ** 0.5
    NS = 10
    GW = D + E
    assert D == 256 and E == 8 and F == 1024 and S % CH == 0

    x = x_in.rearrange("a s d -> (a s) d")
    y_out = out.rearrange("a s d -> (a s) d")
    xs = nc.dram_tensor("routed_rows", [E * REGION + TS, ROW], F32).ap()
    yk = nc.dram_tensor("expert_rows", [K2 * S, D], F32).ap()
    x2d = nc.dram_tensor("x_after_attention", [S, D], F32).ap()

    plan = make_plan(NT)
    chunk0 = [0]
    for i in range(NT):
        chunk0.append(chunk0[-1] + i // 4 + 1)
    KINDS = ("wT", "M", "G", "xT", "qm", "v", "fT", "t", "pre")
    HILO = ("M", "xT", "qm", "v", "fT")
    job, hijob = {}, {}
    for it in plan:
        if it[0] in KINDS:
            job[it] = len(job)
            if it[0] in HILO:
                hijob[it] = len(hijob)

    def width(i, c):
        w = CH if c < i // 4 else (i % 4 + 1) * P
        return w, max(w, 2 * P)

    with ExitStack() as keep:
        def sbk(name, shape, dt):
            return keep.enter_context(nc.sbuf_tensor(name, shape, dt))

        def sem(name):
            return keep.enter_context(nc.semaphore(name))

        ident = sbk("ident", [P, P], F32)
        route_w = sbk("route_w", [P, NT, K2], F32)
        tile_row = sbk("tile_row", [1, NTILES], I32)
        tile_expert = sbk("tile_expert", [1, NTILES], I32)
        pad_row = sbk("pad_row", [1, E], I32)

        with ExitStack() as ctx:
            def sb(name, shape, dt):
                return ctx.enter_context(nc.sbuf_tensor(name, shape, dt))

            ps_s = [ctx.enter_context(nc.psum_tensor(f"ps_s{k}", [P, CH], F32)) for k in range(2)]
            ps_t = [ctx.enter_context(nc.psum_tensor(f"ps_t{k}", [P, CH], F32)) for k in range(2)]
            ps_o = [ctx.enter_context(nc.psum_tensor(f"ps_o{k}", [P, CH], F32)) for k in range(2)]
            ps_m = [ctx.enter_context(nc.psum_tensor(f"ps_m{k}", [P, CH], F32)) for k in range(2)]

            xT = [sb(f"xT{k}", [P, DC, S], F32R) for k in "hl"]
            V = [sb(f"V{k}", [P, NT, D], F32R) for k in "hl"]
            QT = [[sb(f"QT{p}{k}", [P, DC, 2 * P], F32R) for k in "hl"] for p in range(2)]
            PT = [[sb(f"PT{p}{k}", [P, CH], F32R) for k in "hl"] for p in range(2)]
            scores = sb("scores", [P, NS, CH], F32)
            xn = [sb(f"xn{p}", [P, 2, D], F32) for p in range(2)]
            xres = [sb(f"xres{p}", [P, D], F32) for p in range(2)]
            x2 = sb("x2", [P, 2, D], F32)
            xn2 = sb("xn2", [P, 2, D], F32)
            x2T = [sb(f"x2T{k}", [P, DC, 2 * P], F32R) for k in "hl"]
            trow = sb("trow", [P, 2, K2, ROW], F32)
            Mw = [sb(f"Mw{k}", [P, DC, D], F32R) for k in "hl"]
            Vws = [sb(f"Vw{k}", [P, DC, D], F32R) for k in "hl"]
            Wi = [sb(f"Wi{k}", [P, DC, GW], F32R) for k in "hl"]
            causal = sb("causal", [P, CH + P], F32)
            pad = sb("pad", [P, 2, ROW], F32)
            bin_row = sb("bin_row", [P, D], F32)
            bin_col = sb("bin_col", [P, DC], F32)
            wg = sb("wg", [P, DC, E], F32)
            gate_bias = sb("gate_bias", [P, E], F32)
            bgate = sb("bgate", [P, E], F32)
            before = sb("before", [P, P], BF16)
            ones = sb("ones", [P, P], BF16)
            earlier = sb("earlier", [P, E, E], F32)
            target_i = sb("target_i", [P, NT, K2], I32)
            target = sb("target", [P, NT, K2], F32)
            base_i = sb("base_i", [P, E], I32)
            base = sb("base", [P, E], F32)
            tau_i = sb("tau_i", [P, NTILES], I32)
            mxs = sb("mxs", [P, NT, NCH], F32)
            negm = sb("negm", [P, NT], F32)
            lsum = sb("lsum", [P, NT, NCH], F32)
            rden = sb("rden", [P, 2], F32)
            stats = sb("stats", [P, 2, 6], F32)
            mv = sb("mv", [P, 2, 2], F32)
            nw = sb("nw", [P, 3, 2], F32)
            nwi = sb("nwi", [P, 2], I32)
            lg = sb("lg", [P, 2, E], F32)
            cmp = sb("cmp", [P, 2, 2, E, E], F32)
            rank = sb("rank", [P, 2, E], F32)
            pick = [sb(f"pick{k}", [P, 2, E], F32) for k in range(K2)]
            prod = sb("prod", [P, K2, 2, E], F32)
            lk = sb("lk", [P, K2, 2], F32)
            gd = sb("gd", [P, 2], F32)
            ge = sb("ge", [P, 2], F32)
            gs = sb("gs", [P, 2], F32)
            gr = sb("gr", [P, 2], F32)
            sel = sb("sel", [P, 2, E], BF16)
            cnt = sb("cnt", [P, E], F32)
            pos = sb("pos", [P, 2, E], F32)
            posf = sb("posf", [P, 2, K2], F32)
            slot = sb("slot", [P, NT, K2], U32)
            tabe = sb("tabe", [1, 8, E], F32)
            tabi = sb("tabi", [1, E], I32)
            f32 = lambda ap: ap.bitcast(F32)

            wraw = [scores[:, k, :].rearrange("p (c n) -> p c n", c=DC) for k in range(4)]
            wTr = [scores[:, 4 + k, :].rearrange("p (c n) -> p c n", c=DC) for k in range(3)]

            bin_wide = scores[:, 7, 0:DC * P].rearrange("p (c n) -> p c n", c=DC)
            flat = scores[0:1, :, :].rearrange("p s n -> p (s n)")
            tabf = flat[:, 0:4 * NTILES].rearrange("p (k t) -> p k t", k=4)
            oneh = flat[:, CH:CH + 3 * NTILES * E].rearrange("p (k t e) -> p k t e", k=3, e=E)

            w_in = sem("w_in")
            x_ld = [sem(f"x_ld{p}") for p in range(2)]
            res_ld = [sem(f"res_ld{p}") for p in range(2)]
            consts = sem("consts")
            vchain = sem("vchain")
            pchain = sem("pchain")
            ln_done = sem("ln_done")
            ln2_done = sem("ln2_done")
            wcast = sem("wcast")
            wdone = sem("wdone")
            misc_full = sem("misc_full")
            misc_hi = sem("misc_hi")
            misc_done = sem("misc_done")
            scores_full = sem("scores_full")
            scores_out = sem("scores_out")
            max_ready = sem("max_ready")
            exp_done = sem("exp_done")
            pt_full = sem("pt_full")
            pt_hi = sem("pt_hi")
            pt_lo = sem("pt_lo")
            pv_done = sem("pv_done")
            fin_done = sem("fin_done")
            x2_stored = sem("x2_stored")
            gate_diff = sem("gate_diff")
            gate_exp = sem("gate_exp")
            sel_ready = sem("sel_ready")
            slots_ready = sem("slots_ready")
            t_ready = sem("t_ready")
            scattered = sem("scattered")
            tables = sem("tables")
            padded = sem("padded")
            block = ctx.enter_context(nc.Block())

            N_W = 9

            @block.sync
            def _(sp):
                for k, w in enumerate((Qw, Kw, W_in, Vw)):
                    sp.dma_start(wraw[k], w.rearrange("(c p) n -> p c n", p=P)).then_inc(w_in, 16)
                sp.dma_start(wg[:], W_gate.rearrange("(c p) n -> p c n", p=P)).then_inc(w_in, 16)
                sp.dma_start(bin_row[:], rows_bcast(b_in, P)).then_inc(w_in, 16)
                sp.dma_start(bgate[:], rows_bcast(b_gate, P)).then_inc(w_in, 16)
                for c in range(DC):
                    sp.dma_start(bin_col[:, c:c + 1],
                                 b_in[c * P:(c + 1) * P].rearrange("(p a) -> p a", a=1)).then_inc(w_in, 16)
                for it in plan:
                    if it[0] == "ln1":
                        h = it[1]
                        if h >= 2:
                            sp.wait_ge(misc_full, job[("xT", h - 2)] + 1)
                        sp.dma_start(xn[h % 2][:], x[h * 2 * P:(h + 1) * 2 * P, :].rearrange(
                            "(t p) d -> p t d", p=P)).then_inc(x_ld[h % 2], 16)
                    elif it[0] == "mx":
                        i = it[1]
                        if i >= 2:
                            sp.wait_ge(fin_done, i - 1)
                        sp.dma_start(xres[i % 2][:], x[i * P:(i + 1) * P, :]).then_inc(res_ld[i % 2], 16)
                    elif it[0] == "ln2":
                        h = it[1]
                        sp.wait_ge(fin_done, 2 * h + 2)
                        sp.dma_start(x2d[h * 2 * P:(h + 1) * 2 * P, :].rearrange("(t p) d -> p t d", p=P),
                                     x2[:]).then_inc(x2_stored, 16)
                sp.wait_ge(tables, 1)
                sp.dma_start(xs[E * REGION:E * REGION + TS, :].rearrange("(p a) d -> p a d", a=2),
                             pad[:]).then_inc(padded, 16)
                for e in range(E):
                    r = sp.snap(sp.value_load(pad_row[0:1, e:e + 1], min_val=0, max_val=E * REGION - TS))
                    sp.dma_start(xs[bass.ds(r, TS), :].rearrange("(p a) d -> p a d", a=2),
                                 pad[:]).then_inc(padded, 16)
                sp.wait_ge(padded, 16 * (E + 1))
                sp.wait_ge(x2_stored, 16 * NH)

            @block.gpsimd
            def _(pool):
                done = [0]

                def link(ins):
                    done[0] += 1
                    ins.then_inc(pchain, 1)
                    pool.wait_ge(pchain, done[0])

                link(pool.memset(ident[:], 0.0))
                pool.affine_select(out=ident[:], in_=ident[:], compare_op=ALU.not_equal, fill=1.0, base=0,
                                   pattern=[[-1, P]], channel_multiplier=1).then_inc(consts, 1)
                link(pool.memset(causal[:], 0.0))
                pool.affine_select(out=causal[:, CH:], in_=causal[:, CH:], compare_op=ALU.is_ge, fill=NEG,
                                   base=0, pattern=[[-1, P]], channel_multiplier=1).then_inc(consts, 1)
                link(pool.memset(before[:], 0.0))
                pool.affine_select(out=before[:], in_=before[:], compare_op=ALU.is_ge, fill=1.0, base=0,
                                   pattern=[[-1, P]], channel_multiplier=1).then_inc(consts, 1)
                pool.memset(ones[:], 1.0).then_inc(consts, 1)
                link(pool.memset(earlier[:], 0.0))
                pool.affine_select(out=earlier[:], in_=earlier[:], compare_op=ALU.is_ge, fill=1.0, base=0,
                                   pattern=[[-1, E], [1, E]], channel_multiplier=0).then_inc(consts, 1)
                pool.iota(target_i[:], pattern=[[2 * P, NT], [1, K2]], base=0,
                          channel_multiplier=2).then_inc(consts, 1)
                pool.iota(base_i[:], pattern=[[REGION, E]], base=0, channel_multiplier=0).then_inc(consts, 1)
                pool.iota(tau_i[:], pattern=[[1, NTILES]], base=0, channel_multiplier=0).then_inc(consts, 1)
                link(pool.memset(pad[:], 0.0))
                pool.memset(pad[:, :, D:ROW], NOWHERE).then_inc(consts, 1)
                for it in plan:
                    if it[0] == "route":
                        h = it[1]
                        pool.wait_ge(misc_done, job[("t", h, 1)] + 1)
                        for s in range(2):
                            pool.tensor_copy(trow[:, s, 1, 0:D], trow[:, s, 0, 0:D]).then_inc(t_ready, 1)
                        pool.wait_ge(wdone, 1)
                        pool.tensor_copy(trow[:, :, :, D], target[:, 2 * h:2 * h + 2, :]).then_inc(t_ready, 1)
                    elif it[0] == "pre":
                        h = it[1]
                        pool.wait_ge(slots_ready, h + 1)
                        pool.wait_ge(t_ready, 3 * (h + 1))
                        for s in range(2):
                            for k in range(K2):
                                pool.indirect_dma_start(
                                    xs, bass.IndirectOffsetOnAxis(ap=slot[:, 2 * h + s, k:k + 1], axis=0),
                                    trow[:, s, k, :], None, bounds_check=E * REGION - 1).then_inc(scattered, 16)
                pool.wait_ge(scattered, 16 * 2 * K2 * NH)

            @block.scalar
            def _(act):
                act.wait_ge(w_in, 16 * N_W)
                nc.scalar.copy(Vws[0][:], wraw[3]).then_inc(wcast, 1)
                nc.scalar.copy(Wi[0][:, :, 0:D], wraw[2]).then_inc(wcast, 1)

                def hi(it, dst):
                    act.wait_ge(misc_full, job[it] + 1)
                    w = dst.free_size()
                    src = ps_m[job[it] % 2][:, 0:w]
                    if len(dst.shape) == 3:
                        src = src.rearrange("p (c n) -> p c n", c=dst.shape[1])
                    nc.scalar.copy(dst, src).then_inc(misc_hi, 1)

                for it in plan:
                    if it[0] == "M":
                        hi(it, Mw[0][:])
                    elif it[0] == "xT":
                        hi(it, xT[0][:, :, it[1] * 2 * P:(it[1] + 1) * 2 * P])
                    elif it[0] == "qm":
                        hi(it, QT[it[1] % 2][0][:])
                    elif it[0] == "v":
                        hi(it, V[0][:, 2 * it[1]:2 * it[1] + 2, :])
                    elif it[0] == "fT":
                        hi(it, x2T[0][:])
                    elif it[0] == "ex":
                        _, i, c = it
                        g = chunk0[i] + c
                        w, _w = width(i, c)
                        act.wait_ge(max_ready, i + 1)
                        p = scores[:, g % NS, 0:w]
                        nc.scalar.activation(p, p, ACT.Exp, bias=negm[:, i:i + 1], scale=SCALE,
                                             accum_out=lsum[:, i, c:c + 1]).then_inc(exp_done, 1)
                    elif it[0] == "tp":
                        _, i, c = it
                        g = chunk0[i] + c
                        w, _w = width(i, c)
                        act.wait_ge(pt_full, g + 1)
                        if g >= 2:
                            act.wait_ge(pv_done, g - 1)
                        nc.scalar.copy(PT[g % 2][0][:, 0:w], ps_t[g % 2][:, 0:w]).then_inc(pt_hi, 1)
                    elif it[0] == "pre":
                        act.wait_ge(gate_diff, it[1] + 1)
                        nc.scalar.activation(ge[:], gd[:], ACT.Exp).then_inc(gate_exp, 1)

            @block.tensor
            def _(pe):
                def bank(it):
                    n = job[it]
                    if n >= 2:
                        pe.wait_ge(misc_done, n - 1)
                    return ps_m[n % 2]

                pe.wait_ge(w_in, 16 * N_W)
                pe.wait_ge(consts, 9)
                for it in plan:
                    kind = it[0]
                    if kind == "wT":
                        ps = bank(it)
                        for ce in range(DC):
                            for cd in range(DC):
                                at = ce * D + cd * P
                                last = pe.transpose(ps[:, at:at + P], wraw[it[1]][:, cd, ce * P:(ce + 1) * P],
                                                    ident[:])
                        last.then_inc(misc_full, 1)
                    elif kind == "M":
                        pe.wait_ge(misc_done, job[("wT", 1)] + 1)
                        ps = bank(it)
                        for cd in range(DC):
                            for ce in range(DC):
                                last = pe.matmul(ps[:, cd * D:(cd + 1) * D], wTr[0][:, ce, cd * P:(cd + 1) * P],
                                                 wTr[1][:, ce, :], start=(ce == 0), stop=(ce == DC - 1))
                        last.then_inc(misc_full, 1)
                    elif kind == "G":
                        pe.wait_ge(misc_done, job[("wT", 2)] + 1)
                        ps = bank(it)
                        pe.wait_ge(wdone, 2)
                        for cd in range(DC + 1):
                            for ce in range(DC):
                                w = wTr[2][:, ce, cd * P:(cd + 1) * P] if cd < DC else bin_wide[:, ce, :]
                                last = pe.matmul(ps[:, cd * E:(cd + 1) * E], w, wg[:, ce, :],
                                                 start=(ce == 0), stop=(ce == DC - 1))
                        last.then_inc(misc_full, 1)
                    elif kind in ("xT", "fT"):
                        h = it[1]
                        if kind == "xT":
                            pe.wait_ge(ln_done, h + 1)
                        else:
                            pe.wait_ge(ln2_done, h + 1)
                        src = xn[h % 2] if kind == "xT" else xn2
                        ps = bank(it)
                        for s in range(2):
                            for c in range(DC):
                                at = c * 2 * P + s * P
                                last = pe.transpose(ps[:, at:at + P], src[:, s, c * P:(c + 1) * P], ident[:])
                        last.then_inc(misc_full, 1)
                    elif kind == "qm":
                        h = it[1]
                        pe.wait_ge(misc_done, max(job[("xT", h)], job[("M", 0)]) + 1)
                        ps = bank(it)
                        for c2 in range(DC):
                            for c1 in range(DC):
                                last = mm3(pe, ps[:, c2 * D:(c2 + 1) * D],
                                           [m[:, c1, c2 * P:(c2 + 1) * P] for m in Mw],
                                           [t[:, c1, h * 2 * P:(h + 1) * 2 * P] for t in xT],
                                           c1 == 0, c1 == DC - 1)
                        last.then_inc(misc_full, 1)
                    elif kind == "v":
                        h = it[1]
                        pe.wait_ge(wdone, 4)
                        ps = bank(it)
                        for s in range(2):
                            for c in range(DC):
                                at = (2 * h + s) * P
                                last = mm3(pe, ps[:, s * D:(s + 1) * D], [t[:, c, at:at + P] for t in xT],
                                           [w[:, c, :] for w in Vws], c == 0, c == DC - 1)
                        last.then_inc(misc_full, 1)
                    elif kind == "t":
                        _, h, s = it
                        pe.wait_ge(misc_done, job[("fT", h)] + 1)
                        pe.wait_ge(wdone, 6)
                        ps = bank(it)
                        for c in range(DC):
                            last = mm3(pe, ps[:, 0:GW], [t[:, c, s * P:(s + 1) * P] for t in x2T],
                                       [w[:, c, :] for w in Wi], c == 0, c == DC - 1)
                        last.then_inc(misc_full, 1)
                    elif kind == "pre":
                        h = it[1]
                        pe.wait_ge(sel_ready, h + 1)
                        ps = bank(it)
                        s2 = sel[:].rearrange("p t e -> p (t e)")
                        pe.matmul(ps[:, 0:2 * E], before[:], s2, start=True, stop=True)
                        pe.matmul(ps[:, 2 * E:4 * E], ones[:], s2, start=True, stop=True).then_inc(misc_full, 1)
                    elif kind == "qk":
                        _, i, c = it
                        g = chunk0[i] + c
                        w, wide = width(i, c)
                        if c == 0:
                            pe.wait_ge(misc_done, job[("qm", i // 2)] + 1)
                        if g >= 2:
                            pe.wait_ge(scores_out, g - 1)
                        at = (i % 2) * P
                        for d in range(DC):
                            last = mm3(pe, ps_s[g % 2][:, 0:wide], [q[:, d, at:at + P] for q in QT[i // 2 % 2]],
                                       [t[:, d, c * CH:c * CH + wide] for t in xT], d == 0, d == DC - 1)
                        last.then_inc(scores_full, 1)
                    elif kind == "tp":
                        _, i, c = it
                        g = chunk0[i] + c
                        w, _w = width(i, c)
                        pe.wait_ge(exp_done, g + 1)
                        if g >= 2:
                            pe.wait_ge(pt_lo, g - 1)
                        for k in range(w // P):
                            last = pe.transpose(ps_t[g % 2][:, k * P:(k + 1) * P],
                                                scores[:, g % NS, k * P:(k + 1) * P], ident[:])
                        last.then_inc(pt_full, 1)
                    elif kind == "pv":
                        _, i, c = it
                        g = chunk0[i] + c
                        w, _w = width(i, c)
                        pe.wait_ge(pt_lo, g + 1)
                        if c == 0:
                            pe.wait_ge(misc_done, job[("v", i // 2)] + 1)
                            if i >= 2:
                                pe.wait_ge(fin_done, i - 1)
                        for k in range(w // P):
                            kt = c * 4 + k
                            last = mm3(pe, ps_o[i % 2][:, 0:D], [p[:, k * P:(k + 1) * P] for p in PT[g % 2]],
                                       [v[:, kt, :] for v in V], kt == 0, kt == i)
                        last.then_inc(pv_done, 1)

            @block.vector
            def _(dve):
                done = [0]

                def link(ins):
                    done[0] += 1
                    ins.then_inc(vchain, 1)
                    dve.wait_ge(vchain, done[0])

                def layernorm(src, dst, ready):
                    for s in range(2):
                        last = dve.bn_stats(stats[:, s, :], src[:, s, :])
                    link(last)
                    for s in range(2):
                        last = dve.bn_aggr(mv[:, s, :], stats[:, s, :])
                    link(last)
                    v, y, a = nw[:, 0, :], nw[:, 1, :], nw[:, 2, :]
                    link(dve.tensor_scalar(v, mv[:, :, 1], EPS, None, ALU.add))
                    link(dve.tensor_scalar(nwi[:], v.bitcast(I32), 1, None, ALU.logical_shift_right))
                    link(dve.tensor_scalar(y.bitcast(I32), nwi[:], -1.0, float(RSQRT_SEED), ALU.mult, ALU.add))
                    for _ in range(3):
                        link(dve.scalar_tensor_tensor(a, y, -0.5, y, ALU.mult, ALU.mult))
                        link(dve.tensor_tensor(a, a, v, ALU.mult))
                        link(dve.scalar_tensor_tensor(y, a, 1.5, y, ALU.add, ALU.mult))
                    for s in range(2):
                        last = dve.tensor_scalar(dst[:, s, :], src[:, s, :], mv[:, s, 0:1], nw[:, 1, s:s + 1],
                                                 ALU.subtract, ALU.mult)
                    last.then_inc(ready, 1)

                def lo(it, dst, hi_part):
                    dve.wait_ge(misc_hi, hijob[it] + 1)
                    src = ps_m[job[it] % 2][:, 0:dst.free_size()].rearrange("p (c n) -> p c n", c=dst.shape[1])
                    dve.tensor_tensor(dst, src, f32(hi_part), ALU.subtract).then_inc(misc_done, 1)

                dve.wait_ge(consts, 9)
                dve.tensor_copy(target[:], target_i[:]).then_inc(wdone, 1)
                dve.wait_ge(w_in, 16 * N_W)
                last = None
                for c in range(DC):
                    last = dve.tensor_copy(bin_wide[:, c, :], bin_col[:, c:c + 1].to_broadcast([P, P]))
                last.then_inc(wdone, 1)
                dve.tensor_copy(base[:], base_i[:]).then_inc(wdone, 1)
                dve.wait_ge(wdone, 3)
                link(dve.tensor_copy(cnt[:], base[:]))
                dve.wait_ge(wcast, 1)
                dve.tensor_tensor(Vws[1][:], wraw[3], f32(Vws[0][:]), ALU.subtract).then_inc(wdone, 1)
                dve.wait_ge(wcast, 2)
                dve.tensor_tensor(Wi[1][:, :, 0:D], wraw[2], f32(Wi[0][:, :, 0:D]),
                                  ALU.subtract).then_inc(wdone, 1)
                for it in plan:
                    kind = it[0]
                    if kind == "wT":
                        dve.wait_ge(misc_full, job[it] + 1)
                        dve.tensor_copy(wTr[it[1]], ps_m[job[it] % 2][:].rearrange("p (c n) -> p c n", c=DC))\
                           .then_inc(misc_done, 1)
                    elif kind == "M":
                        lo(it, Mw[1][:], Mw[0][:])
                    elif kind == "G":
                        dve.wait_ge(misc_full, job[it] + 1)
                        ps = ps_m[job[it] % 2]
                        g2 = ps[:, 0:DC * E].rearrange("p (c e) -> p c e", c=DC)
                        link(dve.tensor_copy(Wi[0][:, :, D:GW], g2))
                        dve.tensor_tensor(Wi[1][:, :, D:GW], g2, f32(Wi[0][:, :, D:GW]),
                                          ALU.subtract).then_inc(wdone, 1)
                        dve.tensor_tensor(gate_bias[:], ps[:, DC * E:(DC + 1) * E], bgate[:],
                                          ALU.add).then_inc(misc_done, 1)
                        dve.wait_ge(misc_done, job[it] + 1)
                    elif kind == "ln1":
                        h = it[1]
                        dve.wait_ge(x_ld[h % 2], 16 * (h // 2 + 1))
                        layernorm(xn[h % 2], xn[h % 2], ln_done)
                    elif kind == "ln2":
                        layernorm(x2, xn2, ln2_done)
                    elif kind == "xT":
                        at = slice(it[1] * 2 * P, (it[1] + 1) * 2 * P)
                        lo(it, xT[1][:, :, at], xT[0][:, :, at])
                    elif kind == "qm":
                        q = QT[it[1] % 2]
                        lo(it, q[1][:], q[0][:])
                    elif kind == "v":
                        at = slice(2 * it[1], 2 * it[1] + 2)
                        lo(it, V[1][:, at, :], V[0][:, at, :])
                    elif kind == "fT":
                        lo(it, x2T[1][:], x2T[0][:])
                    elif kind == "qk":
                        _, i, c = it
                        g = chunk0[i] + c
                        w, _w = width(i, c)
                        dve.wait_ge(scores_full, g + 1)
                        if g >= NS:
                            dve.wait_ge(pt_full, g - NS + 1)
                        diag = c == i // 4
                        mask = causal[:, CH + P - w:CH + P] if diag else causal[:, 0:w]
                        dve.tensor_tensor_reduce(scores[:, g % NS, 0:w], ps_s[g % 2][:, 0:w], mask, 1.0, NEG,
                                                 ALU.add, ALU.max, mxs[:, i, c:c + 1]).then_inc(scores_out, 1)
                    elif kind == "mx":
                        i = it[1]
                        dve.wait_ge(scores_out, chunk0[i + 1])
                        link(dve.tensor_reduce(negm[:, i:i + 1], mxs[:, i, 0:i // 4 + 1], AX.X, ALU.max))
                        dve.tensor_scalar(negm[:, i:i + 1], negm[:, i:i + 1], -SCALE, None,
                                          ALU.mult).then_inc(max_ready, 1)
                    elif kind == "tp":
                        _, i, c = it
                        g = chunk0[i] + c
                        w, _w = width(i, c)
                        dve.wait_ge(pt_hi, g + 1)
                        dve.tensor_tensor(PT[g % 2][1][:, 0:w], ps_t[g % 2][:, 0:w],
                                          f32(PT[g % 2][0][:, 0:w]), ALU.subtract).then_inc(pt_lo, 1)
                    elif kind == "fin":
                        i = it[1]
                        dve.wait_ge(pv_done, chunk0[i + 1])
                        link(dve.tensor_reduce(rden[:, 0:1], lsum[:, i, 0:i // 4 + 1], AX.X, ALU.add))
                        link(dve.reciprocal(rden[:, 1:2], rden[:, 0:1]))
                        dve.wait_ge(res_ld[i % 2], 16 * (i // 2 + 1))
                        if i % 2 == 0 and i >= 2:
                            dve.wait_ge(x2_stored, 16 * (i // 2))
                        dve.scalar_tensor_tensor(x2[:, i % 2, :], ps_o[i % 2][:, 0:D], rden[:, 1:2],
                                                 xres[i % 2][:], ALU.mult, ALU.add).then_inc(fin_done, 1)
                        dve.wait_ge(fin_done, i + 1)
                    elif kind == "t":
                        _, h, s = it
                        if s == 0 and h >= 1:
                            dve.wait_ge(scattered, 16 * 2 * K2 * h)
                        dve.wait_ge(misc_full, job[it] + 1)
                        ps = ps_m[job[it] % 2]
                        dve.tensor_tensor(trow[:, s, 0, 0:D], ps[:, 0:D], bin_row[:], ALU.add)
                        dve.tensor_tensor(lg[:, s, :], ps[:, D:GW], gate_bias[:], ALU.add)\
                           .then_inc(misc_done, 1)
                    elif kind == "route":
                        h = it[1]
                        dve.wait_ge(misc_done, job[("t", h, 1)] + 1)
                        lj = lg[:].unsqueeze(2).to_broadcast([P, 2, E, E])
                        le = lg[:].unsqueeze(3).to_broadcast([P, 2, E, E])
                        dve.tensor_tensor(cmp[:, 0], lj, le, ALU.is_gt)
                        link(dve.tensor_tensor(cmp[:, 1], lj, le, ALU.is_equal))
                        link(dve.tensor_tensor(cmp[:, 1], cmp[:, 1],
                                               earlier[:].unsqueeze(1).to_broadcast([P, 2, E, E]), ALU.mult))
                        link(dve.tensor_tensor(cmp[:, 0], cmp[:, 0], cmp[:, 1], ALU.add))
                        link(dve.tensor_reduce(rank[:], cmp[:, 0], AX.X, ALU.add))
                        dve.tensor_scalar(sel[:], rank[:], float(K2), None, ALU.is_lt).then_inc(sel_ready, 1)
                        for k in range(K2):
                            last = dve.tensor_scalar(pick[k][:], rank[:], float(k), None, ALU.is_equal)
                        link(last)
                        for k in range(K2):
                            last = dve.tensor_tensor(prod[:, k], pick[k][:], lg[:], ALU.mult)
                        link(last)
                        link(dve.tensor_reduce(lk[:], prod[:], AX.X, ALU.add))
                        dve.tensor_tensor(gd[:], lk[:, 1, :], lk[:, 0, :], ALU.subtract).then_inc(gate_diff, 1)
                    elif kind == "pre":
                        h = it[1]
                        dve.wait_ge(misc_full, job[it] + 1)
                        ps = ps_m[job[it] % 2]
                        dve.tensor_tensor(pos[:, 0, :], ps[:, 0:E], cnt[:], ALU.add)
                        link(dve.tensor_tensor(cnt[:], ps[:, 2 * E:3 * E], cnt[:], ALU.add))
                        dve.tensor_tensor(pos[:, 1, :], ps[:, E:2 * E], cnt[:], ALU.add)
                        dve.tensor_tensor(cnt[:], ps[:, 3 * E:4 * E], cnt[:], ALU.add).then_inc(misc_done, 1)
                        dve.wait_ge(misc_done, job[it] + 1)
                        for k in range(K2):
                            last = dve.tensor_tensor(prod[:, k], pick[k][:], pos[:], ALU.mult)
                        link(last)
                        for k in range(K2):
                            last = dve.tensor_reduce(posf[:, :, k], prod[:, k], AX.X, ALU.add)
                        link(last)
                        dve.tensor_copy(slot[:, 2 * h:2 * h + 2, :], posf[:]).then_inc(slots_ready, 1)
                        dve.wait_ge(gate_exp, h + 1)
                        link(dve.tensor_scalar(gs[:], ge[:], 1.0, None, ALU.add))
                        link(dve.reciprocal(gr[:], gs[:]))
                        dve.tensor_copy(route_w[:, 2 * h:2 * h + 2, 0], gr[:])
                        link(dve.tensor_tensor(route_w[:, 2 * h:2 * h + 2, 1], gr[:], ge[:], ALU.mult))

                rowf, expf, used, tau = (tabf[:, k, :] for k in range(4))
                cnt0, n, tiles, incl, excl, tmp, delta = (tabe[:, k, :] for k in range(7))
                link(dve.tensor_copy(cnt0, cnt[0:1, :]))
                link(dve.tensor_copy(pad_row[:], cnt0))
                link(dve.tensor_tensor(n, cnt0, base[0:1, :], ALU.subtract))
                link(dve.tensor_scalar(tmp, n, float(TS - 1), None, ALU.add))
                link(dve.tensor_copy(tabi[:], tmp))
                link(dve.tensor_scalar(tabi[:], tabi[:], TS.bit_length() - 1, None, ALU.logical_shift_right))
                link(dve.tensor_copy(tiles, tabi[:]))
                link(dve.tensor_copy(incl, tiles))
                for e in range(1, E):
                    link(dve.tensor_tensor(incl[:, e:e + 1], incl[:, e - 1:e], tiles[:, e:e + 1], ALU.add))
                link(dve.tensor_tensor(excl, incl, tiles, ALU.subtract))
                link(dve.scalar_tensor_tensor(delta, excl, -float(TS), base[0:1, :], ALU.mult, ALU.add))
                link(dve.tensor_copy(tau, tau_i[0:1, :]))
                sh = [1, NTILES, E]
                tb = tau.unsqueeze(2).to_broadcast(sh)
                link(dve.tensor_tensor(oneh[:, 0], tb, incl.unsqueeze(1).to_broadcast(sh), ALU.is_ge))
                link(dve.tensor_tensor(oneh[:, 1], tb, excl.unsqueeze(1).to_broadcast(sh), ALU.is_ge))
                link(dve.tensor_reduce(expf, oneh[:, 0], AX.X, ALU.add))
                link(dve.tensor_tensor(oneh[:, 2], oneh[:, 1], oneh[:, 0], ALU.subtract))
                link(dve.tensor_tensor(oneh[:, 1], oneh[:, 2], delta.unsqueeze(1).to_broadcast(sh), ALU.mult))
                link(dve.tensor_reduce(rowf, oneh[:, 1], AX.X, ALU.add))
                link(dve.scalar_tensor_tensor(rowf, tau, float(TS), rowf, ALU.mult, ALU.add))
                link(dve.tensor_scalar(used, expf, float(E) - 0.5, None, ALU.is_lt))
                link(dve.scalar_tensor_tensor(rowf, rowf, -float(E * REGION), used, ALU.add, ALU.mult))
                link(dve.tensor_scalar(rowf, rowf, float(E * REGION), None, ALU.add))
                link(dve.tensor_scalar(expf, expf, float(E - 1), None, ALU.min))
                link(dve.tensor_copy(tile_row[:], rowf))
                dve.tensor_copy(tile_expert[:], expf).then_inc(tables, 1)

        with ExitStack() as ctx:
            def sb(name, shape, dt):
                return ctx.enter_context(nc.sbuf_tensor(name, shape, dt))

            ps_x = ctx.enter_context(nc.psum_tensor("ps_x", [P, CH], F32))
            NHB = 3
            ps_h = [ctx.enter_context(nc.psum_tensor(f"ps_h{k}", [P, CH], F32)) for k in range(NHB)]
            ps_e = [[ctx.enter_context(nc.psum_tensor(f"ps_e{p}{s}", [P, CH], F32)) for s in range(2)]
                    for p in range(2)]
            HQ = HC // 2
            xr = [sb(f"xr{p}", [P, 2, ROW], F32) for p in range(2)]
            w1r = [sb(f"w1r{p}", [P, DC, F], F32) for p in range(2)]
            w2r = [sb(f"w2r{p}", [P, HC, D], F32) for p in range(2)]
            b1s = [sb(f"b1s{p}", [P, HC], F32) for p in range(2)]
            b2s = [sb(f"b2s{p}", [P, D], F32) for p in range(2)]
            w1 = [[sb(f"w1{p}{k}", [P, DC, HC, P], F32R) for k in "hl"] for p in range(2)]
            w2 = [[sb(f"w2{p}{k}", [P, HC, D], F32R) for k in "hl"] for p in range(2)]
            xrT = [sb(f"xrT{k}", [P, DC, TS], F32R) for k in "hl"]
            mid = sb("mid", [P, HC, TS], F32)
            midT = [sb(f"midT{k}", [P, HC, TS], F32R) for k in "hl"]
            esb = [sb(f"esb{p}", [P, 2, D], F32) for p in range(2)]
            eidx = [sb(f"eidx{p}", [P, 2], U32) for p in range(2)]
            f32 = lambda ap: ap.bitcast(F32)

            in_x = [sem(f"in_x{p}") for p in range(2)]
            in_w1 = [sem(f"in_w1{p}") for p in range(2)]
            in_w2 = [sem(f"in_w2{p}") for p in range(2)]
            in_b = [sem(f"in_b{p}") for p in range(2)]
            xt_full = sem("xt_full")
            xt_hi = sem("xt_hi")
            xt_lo = sem("xt_lo")
            w1_hi = sem("w1_hi")
            w1_lo = sem("w1_lo")
            w2_hi = sem("w2_hi")
            w2_lo = sem("w2_lo")
            hid_full = sem("hid_full")
            relu_done = sem("relu_done")
            mid_hi = sem("mid_hi")
            mid_lo = sem("mid_lo")
            h1_done = sem("h1_done")
            e_full = sem("e_full")
            e_out = sem("e_out")
            idx_done = sem("idx_done")
            e_stored = [sem(f"e_stored{p}") for p in range(2)]
            block = ctx.enter_context(nc.Block())

            def over_tiles(eng, body, first):
                n = (NTILES - first) // 2
                with eng.Fori(0, n) as j:
                    for k in range(2):
                        body(j * 2 + (first + k), (first + k) % 2)
                for t in range(first + 2 * n, NTILES):
                    body(t, t % 2)

            def half(t):
                return t // 2

            @block.sync
            def _(sp):
                def load(t, p, head):
                    r = sp.snap(sp.value_load(tile_row[0:1, bass.ds(t, 1)], min_val=0, max_val=E * REGION))
                    e = sp.snap(sp.value_load(tile_expert[0:1, bass.ds(t, 1)], min_val=0, max_val=E - 1))
                    if not head:
                        done = sp.snap(t - 1)
                        q1 = sp.snap(DC * (t - 1))
                        q2 = sp.snap(HQ * (t - 1))
                        sp.wait_ge(xt_full, done)
                        sp.wait_ge(idx_done, done)
                    sp.dma_start(xr[p][:], xs[bass.ds(r, TS), :].rearrange("(a q) d -> q a d", q=P))\
                      .then_inc(in_x[p], 16)
                    if not head:
                        sp.wait_ge(w1_lo, q1)
                    sp.dma_start(w1r[p][:], W1[bass.ds(e, 1), :, :].rearrange("a (c q) n -> q (a c) n", q=P))\
                      .then_inc(in_w1[p], 16)
                    if not head:
                        sp.wait_ge(w2_lo, q2)
                    sp.dma_start(w2r[p][:], W2[bass.ds(e, 1), :, :].rearrange("a (q c) n -> q (a c) n", c=HC))\
                      .then_inc(in_w2[p], 16)
                    if not head:
                        sp.wait_ge(e_out, done)
                    sp.dma_start(b1s[p][:], b1[bass.ds(e, 1), :].rearrange("a (q c) -> q (a c)", c=HC))\
                      .then_inc(in_b[p], 16)
                    sp.dma_start(b2s[p][:], b2[bass.ds(e, 1), :].partition_broadcast(P).rearrange(
                        "q a n -> q (a n)")).then_inc(in_b[p], 16)

                load(0, 0, True)
                load(1, 1, True)
                over_tiles(sp, lambda t, p: load(t, p, False), 2)

            @block.gpsimd
            def _(pool):
                def store(t, p, head):
                    if not head:
                        pool.wait_ge(e_stored[p], 32 * half(t))
                    pool.wait_ge(in_x[p], 16 * (half(t) + 1))
                    pool.tensor_copy(eidx[p][:], xr[p][:, :, D]).then_inc(idx_done, 1)
                    pool.wait_ge(idx_done, t + 1)
                    pool.wait_ge(e_out, t + 1)
                    for s in range(2):
                        pool.indirect_dma_start(
                            yk, bass.IndirectOffsetOnAxis(ap=eidx[p][:, s:s + 1], axis=0), esb[p][:, s, :], None,
                            bounds_check=K2 * S - 1, oob_is_err=False).then_inc(e_stored[p], 16)

                for t in range(NTILES):
                    store(t, t % 2, t < 2)
                for p in range(2):
                    pool.wait_ge(e_stored[p], 32 * ((NTILES - p + 1) // 2))

            @block.scalar
            def _(act):
                def split_w1(t, p, c):
                    if c == 0:
                        act.wait_ge(in_w1[p], 16 * (half(t) + 1))
                    nc.scalar.copy(w1[p][0][:, c].rearrange("q h m -> q m h"),
                                   w1r[p][:, c, :].rearrange("q (m h) -> q m h", h=HC)).then_inc(w1_hi, 1)

                def split_w2(t, p, q):
                    if q == 0:
                        act.wait_ge(in_w2[p], 16 * (half(t) + 1))
                    nc.scalar.copy(w2[p][0][:, 2 * q:2 * q + 2, :], w2r[p][:, 2 * q:2 * q + 2, :]).then_inc(w2_hi, 1)

                def rows_hi(t):
                    act.wait_ge(xt_full, t + 1)
                    nc.scalar.copy(xrT[0][:], ps_x[:].rearrange("q (c n) -> q c n", c=DC)).then_inc(xt_hi, 1)

                def tile(t, p, last):
                    for q in range(HQ):
                        if q == 0:
                            act.wait_ge(in_b[p], 32 * (half(t) + 1))
                        act.wait_ge(hid_full, t * HQ + (q + 1))
                        for k in range(2):
                            h = 2 * q + k
                            r = nc.scalar.activation(mid[:, h, :], ps_h[q % 2][:, k * TS:(k + 1) * TS], ACT.Relu,
                                                     bias=b1s[p][:, h:h + 1])
                        r.then_inc(relu_done, 1)
                        if not last and q < DC:
                            split_w1(t + 1, 1 - p, q)
                    if not last:
                        rows_hi(t + 1)
                        for q in range(HQ):
                            split_w2(t + 1, 1 - p, q)

                for c in range(DC):
                    split_w1(0, 0, c)
                rows_hi(0)
                for q in range(HQ):
                    split_w2(0, 0, q)
                n = (NTILES - 1) // 2
                with act.Fori(0, n) as j:
                    for k in range(2):
                        tile(j * 2 + k, k, False)
                for t in range(2 * n, NTILES):
                    tile(t, t % 2, t == NTILES - 1)

            @block.tensor
            def _(pe):
                def rows(t, p, head):
                    if not head:
                        pe.wait_ge(xt_lo, t)
                    pe.wait_ge(in_x[p], 16 * (half(t) + 1))
                    for s in range(2):
                        for c in range(DC):
                            at = c * TS + s * P
                            last = pe.transpose(ps_x[:, at:at + P], xr[p][:, s, c * P:(c + 1) * P], ident[:])
                    last.then_inc(xt_full, 1)

                def tile(t, p, first, head, last_tile):
                    for q in range(HQ):
                        if not first:
                            pe.wait_ge(relu_done, t * HQ + (q - 1))
                        elif q >= 2:
                            pe.wait_ge(relu_done, q - 1)
                        if q == 0:
                            pe.wait_ge(xt_lo, t + 1)
                            pe.wait_ge(w1_lo, DC * (t + 1))
                        for k in range(2):
                            h = 2 * q + k
                            for c in range(DC):
                                last = mm3(pe, ps_h[q % 2][:, k * TS:(k + 1) * TS], [w[:, c, h, :] for w in w1[p]],
                                           [x_[:, c, :] for x_ in xrT], c == 0, c == DC - 1)
                        last.then_inc(hid_full, 1)
                    if not last_tile:
                        rows(t + 1, 1 - p, False)
                    for q in range(HQ):
                        pe.wait_ge(mid_lo, t * HQ + (q + 1))
                        if q == 0:
                            pe.wait_ge(w2_lo, HQ * (t + 1))
                            if not head:
                                pe.wait_ge(e_out, t - 1)
                        for h in (2 * q, 2 * q + 1):
                            for s in range(2):
                                last = mm3(pe, ps_e[p][s][:, 0:D], [m[:, h, s * P:(s + 1) * P] for m in midT],
                                           [w[:, h, :] for w in w2[p]], h == 0, h == HC - 1)
                    last.then_inc(e_full, 1)

                rows(0, 0, True)
                tile(0, 0, True, True, False)
                tile(1, 1, False, True, False)
                n = (NTILES - 3) // 2
                with pe.Fori(0, n) as j:
                    for k in range(2):
                        tile(j * 2 + (k + 2), k, False, False, False)
                for t in range(2 + 2 * n, NTILES):
                    tile(t, t % 2, False, False, t == NTILES - 1)

            @block.vector
            def _(dve):
                def split_w1(t, p, c):
                    dve.wait_ge(w1_hi, DC * t + (c + 1))
                    dve.tensor_tensor(w1[p][1][:, c].rearrange("q h m -> q m h"),
                                      w1r[p][:, c, :].rearrange("q (m h) -> q m h", h=HC),
                                      f32(w1[p][0][:, c]).rearrange("q h m -> q m h"),
                                      ALU.subtract).then_inc(w1_lo, 1)

                def split_w2(t, p, q):
                    dve.wait_ge(w2_hi, HQ * t + (q + 1))
                    at = slice(2 * q, 2 * q + 2)
                    dve.tensor_tensor(w2[p][1][:, at, :], w2r[p][:, at, :], f32(w2[p][0][:, at, :]),
                                      ALU.subtract).then_inc(w2_lo, 1)

                def rows_lo(t):
                    dve.wait_ge(xt_hi, t + 1)
                    dve.tensor_tensor(xrT[1][:], ps_x[:].rearrange("q (c n) -> q c n", c=DC), f32(xrT[0][:]),
                                      ALU.subtract).then_inc(xt_lo, 1)

                def tile(t, p, head, last):
                    for q in range(HQ):
                        at = slice(2 * q, 2 * q + 2)
                        dve.wait_ge(relu_done, t * HQ + (q + 1))
                        dve.tensor_copy(midT[0][:, at, :], mid[:, at, :]).then_inc(mid_hi, 1)
                        dve.wait_ge(mid_hi, t * HQ + (q + 1))
                        dve.tensor_tensor(midT[1][:, at, :], mid[:, at, :], f32(midT[0][:, at, :]),
                                          ALU.subtract).then_inc(mid_lo, 1)
                        if not last and q < DC:
                            split_w1(t + 1, 1 - p, q)
                    if not last:
                        rows_lo(t + 1)
                        for q in range(HQ):
                            split_w2(t + 1, 1 - p, q)
                    if not head:
                        dve.wait_ge(e_stored[p], 32 * half(t))
                    dve.wait_ge(e_full, t + 1)
                    for s in range(2):
                        r = dve.tensor_tensor(esb[p][:, s, :], ps_e[p][s][:, 0:D], b2s[p][:], ALU.add)
                    r.then_inc(e_out, 1)

                for c in range(DC):
                    split_w1(0, 0, c)
                rows_lo(0)
                for q in range(HQ):
                    split_w2(0, 0, q)
                tile(0, 0, True, False)
                tile(1, 1, True, False)
                n = (NTILES - 3) // 2
                with dve.Fori(0, n) as j:
                    for k in range(2):
                        tile(j * 2 + (k + 2), k, False, False)
                for t in range(2 + 2 * n, NTILES):
                    tile(t, t % 2, False, t == NTILES - 1)

        with ExitStack() as ctx:
            def sb(name, shape, dt):
                return ctx.enter_context(nc.sbuf_tensor(name, shape, dt))

            NB = 4
            ps_c = [ctx.enter_context(nc.psum_tensor(f"ps_c{k}", [P, CH], F32)) for k in range(2)]
            ps_y = [ctx.enter_context(nc.psum_tensor(f"ps_y{k}", [P, CH], F32)) for k in range(2)]
            wor = sb("wor", [P, DC, D], F32)
            wo = [sb(f"wo{k}", [P, DC, D], F32R) for k in "hl"]
            bo = sb("bo", [P, D], F32)
            yt = [sb(f"yt{p}", [P, K2, D], F32) for p in range(NB)]
            xt = [sb(f"xt{p}", [P, D], F32) for p in range(NB)]
            part = [sb(f"part{p}", [P, D], F32) for p in range(2)]
            moe = [sb(f"moe{p}", [P, D], F32) for p in range(2)]
            moeT = [[sb(f"moeT{p}{k}", [P, DC, P], F32R) for k in "hl"] for p in range(2)]
            res = [sb(f"res{p}", [P, D], F32) for p in range(2)]
            f32 = lambda ap: ap.bitcast(F32)
            wo_in = sem("wo_in")
            wo_hi = sem("wo_hi")
            wo_lo = sem("wo_lo")
            y_in = [sem(f"y_in{p}") for p in range(NB)]
            part_done = sem("part_done")
            moe_done = sem("moe_done")
            xb_done = sem("xb_done")
            mt_full = sem("mt_full")
            mt_hi = sem("mt_hi")
            mt_lo = sem("mt_lo")
            y_full = sem("y_full")
            res_done = sem("res_done")
            stored = [sem(f"stored{p}") for p in range(2)]
            block = ctx.enter_context(nc.Block())

            @block.sync
            def _(sp):
                sp.dma_start(wor[:], W_out.rearrange("(c p) n -> p c n", p=P)).then_inc(wo_in, 16)
                sp.dma_start(bo[:], rows_bcast(b_out, P)).then_inc(wo_in, 16)
                for i in range(NT):
                    b = i % NB
                    if i >= NB:
                        sp.wait_ge(res_done, i - NB + 1)
                    at = slice(i * P, (i + 1) * P)
                    sp.dma_start(yt[b][:], yk[K2 * i * P:K2 * (i + 1) * P, :].rearrange(
                        "(p k) d -> p k d", k=K2)).then_inc(y_in[b], 16)
                    sp.dma_start(xt[b][:], x2d[at, :]).then_inc(y_in[b], 16)

            @block.gpsimd
            def _(pool):
                pool.wait_ge(wo_in, 32)
                for i in range(NT):
                    pool.wait_ge(y_in[i % NB], 32 * (i // NB + 1))
                    pool.tensor_tensor(xt[i % NB][:], xt[i % NB][:], bo[:], ALU.add).then_inc(xb_done, 1)

            @block.scalar
            def _(act):
                act.wait_ge(wo_in, 32)
                nc.scalar.copy(wo[0][:], wor[:]).then_inc(wo_hi, 1)
                for i in range(NT + 1):
                    if i < NT:
                        act.wait_ge(mt_full, i + 1)
                        if i >= 2:
                            act.wait_ge(y_full, i - 1)
                        nc.scalar.copy(moeT[i % 2][0][:], ps_c[i % 2][:, 0:D].rearrange(
                            "p (c n) -> p c n", c=DC)).then_inc(mt_hi, 1)
                    if i >= 1:
                        k = i - 1
                        act.wait_ge(res_done, k + 1)
                        act.dma_start(y_out[k * P:(k + 1) * P, :], res[k % 2][:]).then_inc(stored[k % 2], 16)
                for p in range(2):
                    act.wait_ge(stored[p], 16 * (NT // 2))

            @block.tensor
            def _(pe):
                for i in range(NT + 1):
                    if i < NT:
                        pe.wait_ge(moe_done, i + 1)
                        if i >= 2:
                            pe.wait_ge(mt_lo, i - 1)
                        for c in range(DC):
                            last = pe.transpose(ps_c[i % 2][:, c * P:(c + 1) * P], moe[i % 2][:, c * P:(c + 1) * P],
                                                ident[:])
                        last.then_inc(mt_full, 1)
                    if i >= 1:
                        k = i - 1
                        pe.wait_ge(mt_lo, k + 1)
                        if k == 0:
                            pe.wait_ge(wo_lo, 1)
                        if k >= 2:
                            pe.wait_ge(res_done, k - 1)
                        for c in range(DC):
                            last = mm3(pe, ps_y[k % 2][:, 0:D], [m[:, c, :] for m in moeT[k % 2]],
                                       [w[:, c, :] for w in wo], c == 0, c == DC - 1)
                        last.then_inc(y_full, 1)

            @block.vector
            def _(dve):
                dve.wait_ge(wo_hi, 1)
                dve.tensor_tensor(wo[1][:], wor[:], f32(wo[0][:]), ALU.subtract).then_inc(wo_lo, 1)

                def weigh(i):
                    b = i % NB
                    dve.wait_ge(y_in[b], 32 * (i // NB + 1))
                    dve.tensor_scalar(part[i % 2][:], yt[b][:, 0, :], route_w[:, i, 0:1], None,
                                      ALU.mult).then_inc(part_done, 1)
                    if i >= 2:
                        dve.wait_ge(mt_full, i - 1)
                    dve.wait_ge(part_done, i + 1)
                    dve.scalar_tensor_tensor(moe[i % 2][:], yt[b][:, 1, :], route_w[:, i, 1:2], part[i % 2][:],
                                             ALU.mult, ALU.add).then_inc(moe_done, 1)

                weigh(0)
                for i in range(NT + 1):
                    if i + 1 < NT:
                        weigh(i + 1)
                    if i < NT:
                        dve.wait_ge(mt_hi, i + 1)
                        dve.tensor_tensor(moeT[i % 2][1][:], ps_c[i % 2][:, 0:D].rearrange(
                            "p (c n) -> p c n", c=DC), f32(moeT[i % 2][0][:]), ALU.subtract).then_inc(mt_lo, 1)
                    if i >= 1:
                        k = i - 1
                        dve.wait_ge(y_full, k + 1)
                        dve.wait_ge(xb_done, k + 1)
                        if k >= 2:
                            dve.wait_ge(stored[k % 2], 16 * (k // 2))
                        dve.tensor_tensor(res[k % 2][:], ps_y[k % 2][:, 0:D], xt[k % NB][:],
                                          ALU.add).then_inc(res_done, 1)


_INS = ['L0_attn_x', 'L0_attn_Qw', 'L0_attn_Kw', 'L0_attn_Vw', 'L0_ffn_W_in', 'L0_ffn_b_in', 'L0_ffn_W_gate',
        'L0_ffn_b_gate', 'L0_ffn_W1', 'L0_ffn_b1', 'L0_ffn_W2', 'L0_ffn_b2', 'L0_ffn_W_out', 'L0_ffn_b_out']
_OUTS = [((1, 4096, 256), 'float32')]


def kernel(**inputs):
    import numpy as _np
    import concourse.bacc as _bacc
    from concourse import mybir as _mybir
    from concourse.bass_utils import run_bass_kernel_spmd as _run

    nc = _bacc.Bacc("TRN2", target_bir_lowering=False, num_devices=1)
    arrays, args = {}, []
    for name in _INS:
        a = _np.ascontiguousarray(inputs[name])
        arrays[f"in_{name}_dram"] = a
        args.append(nc.dram_tensor(f"in_{name}_dram", a.shape, _mybir.dt.from_np(a.dtype), kind="ExternalInput").ap())
    for i, (shape, dtype) in enumerate(_OUTS):
        dt = _mybir.dt.from_np(_np.dtype(dtype))
        args.append(nc.dram_tensor(f"out_{i}_dram", shape, dt, kind="ExternalOutput").ap())
    build_kernel(nc, *args)
    r = _run(nc, [arrays], core_ids=[0])
    got = tuple(r.results[0][f"out_{i}_dram"] for i in range(len(_OUTS)))
    return got[0]
```

```python
from contextlib import ExitStack

import concourse.bass as bass
from concourse import mybir

F32 = mybir.dt.float32
F32R = mybir.dt.float32r
BF16 = mybir.dt.bfloat16
I32 = mybir.dt.int32
U32 = mybir.dt.uint32
ALU = mybir.AluOpType
ACT = mybir.ActivationFunctionType
AX = mybir.AxisListType

P = 128
EPS = 1e-5
NEG = -3.0e38
RSQRT_SEED = 0x5F3759DF


def rows_bcast(dram, n):
    return dram.rearrange("(a n) -> a n", a=1).partition_broadcast(n).rearrange("p a n -> p (a n)")


def mm3(pe, out, w, m, start, stop):
    pe.matmul(out, w[0], m[0], start=start, stop=False)
    pe.matmul(out, w[0], m[1], start=False, stop=False)
    return pe.matmul(out, w[1], m[0], start=False, stop=stop)


def make_plan(NT):
    NH = NT // 2
    nc_of = lambda i: i // 4 + 1
    plan = [("wT", 0), ("ln1", 0, 0), ("ln1", 0, 1), ("wT", 1), ("ln1", 0, 2), ("M", 0), ("xT", 0), ("Vw", 0),
            ("ln1", 1, 0), ("ln1", 1, 1), ("qm", 0), ("ln1", 1, 2), ("v", 0)]
    groups = [[g(h) for g in group] for h in range(NH) for group in (
        [lambda h: ("ln2", h, 0)],
        [lambda h: ("ln2", h, 1)],
        [lambda h: ("ln2", h, 2)],
        [lambda h: ("fT", h)],
        [lambda h: ("t", h, 0), lambda h: ("t", h, 1)],
        [lambda h: ("route", h, 0)], [lambda h: ("route", h, 1)],
        [lambda h: ("route", h, 2), lambda h: ("pre", h)],
        [lambda h: ("place", h, 0), lambda h: ("place", h, 1), lambda h: ("place", h, 2)])]
    fins, loads, last_fT = 0, 0, -1

    def ffn_group():
        nonlocal loads, last_fT
        out = []
        if groups and (groups[0][0][0] != "ln2" or groups[0][0][1] < loads):
            out = groups.pop(0)
            if out[0][0] == "fT":
                last_fT = out[0][1]
        if loads < NH and 2 * loads + 1 < fins and loads - 1 <= last_fT:
            out = out + [("ld2", loads)]
            loads += 1
        return out

    late = [("Wi", 0), ("wT", 2), ("G", 0)]
    next_b, last_pv, finished = 0, None, []
    s = 0
    while next_b < NT or groups or finished:
        scores = [("qk", s, c) for c in range(nc_of(s))] if s < NT else []
        exps = []
        if 1 <= s <= NT:
            plan.append(("mx", s - 1))
            exps = [("ex", s - 1, c) for c in range(nc_of(s - 1))]
            plan += exps[:2]
            exps = exps[2:]
        if scores:
            plan.append(scores.pop(0))
        if last_pv:
            plan.append(last_pv)
            last_pv = None
        plan += [("fin", i) for i in finished]
        fins += len(finished)
        ahead = []
        k = s // 2 + 1
        if k < NH:
            ahead = [("xT", k)] if s % 2 == 0 else [("qm", k), ("v", k)]
        if k + 1 < NH:
            if s % 2 == 0:
                ahead = ahead + [("ln1", k + 1, 0)]
            else:
                ahead = [("ln1", k + 1, 1), ahead[0], ("ln1", k + 1, 2), ahead[1]]
        last_b = min(s - (2 if s < 12 else 1), NT - 1)
        slots = [(j, c) for j in range(next_b, last_b + 1) for c in range(nc_of(j))]
        finished = list(range(next_b, last_b + 1))
        next_b = max(next_b, last_b + 1)
        placed = 0
        for n, (j, c) in enumerate(slots):
            if scores:
                plan.append(scores.pop(0))
            plan.append(("tp", j, c))
            if exps:
                plan.append(exps.pop(0))
            upto = (n + 1) * len(ahead) // len(slots)
            plan += ahead[placed:upto]
            if last_pv:
                plan.append(last_pv)
            last_pv = ("pv", j, c)
            plan += ffn_group()
            placed = upto
        plan += ahead[placed:] + scores + exps
        if not slots:
            plan += ffn_group()
        plan += late[:1]
        late = late[1:]
        s += 1
    return plan


def build_kernel(nc, x_in, Qw, Kw, Vw, W_in, b_in, W_gate, b_gate, W1, b1, W2, b2, W_out, b_out, out):
    S, D = x_in.shape[1], x_in.shape[2]
    E, F = W1.shape[0], W1.shape[2]
    K2 = 2
    NT = S // P
    NH = NT // 2
    DC = D // P
    CH = 4 * P
    NCH = S // CH
    HC = F // P
    TS = 2 * P
    REGION = S + TS
    NTILES = (K2 * S + E * (TS - 1)) // TS
    ROW = D + 1
    NOWHERE = 1.0e6
    SCALE = 1.0 / float(D) ** 0.5
    NS = 10
    GW = D + E
    assert D == 256 and E == 8 and F == 1024 and S % CH == 0

    x = x_in.rearrange("a s d -> (a s) d")
    y_out = out.rearrange("a s d -> (a s) d")
    xs = nc.dram_tensor("routed_rows", [E * REGION + TS, ROW], F32).ap()
    yk = nc.dram_tensor("expert_rows", [K2 * S, D], F32).ap()
    x2d = nc.dram_tensor("x_after_attention", [S, D], F32).ap()

    plan = make_plan(NT)
    chunk0 = [0]
    for i in range(NT):
        chunk0.append(chunk0[-1] + i // 4 + 1)
    KINDS = ("wT", "M", "G", "xT", "qm", "v", "fT", "t", "pre")
    HILO = ("M", "xT", "qm", "v", "fT")
    job, hijob = {}, {}
    for it in plan:
        if it[0] in KINDS:
            job[it] = len(job)
            if it[0] in HILO:
                hijob[it] = len(hijob)

    def width(i, c):
        w = CH if c < i // 4 else (i % 4 + 1) * P
        return w, max(w, 2 * P)

    with ExitStack() as keep:
        def sbk(name, shape, dt):
            return keep.enter_context(nc.sbuf_tensor(name, shape, dt))

        def sem(name):
            return keep.enter_context(nc.semaphore(name))

        ident = sbk("ident", [P, P], F32)
        route_w = sbk("route_w", [P, NT, K2], F32)
        tile_row = sbk("tile_row", [1, NTILES], I32)
        tile_expert = sbk("tile_expert", [1, NTILES], I32)
        pad_row = sbk("pad_row", [1, E], I32)
        scores = sbk("scores", [P, NS, CH], F32)
        assert DC * F == HC * D == 4 * CH and NS >= 10
        w1r0 = scores[:, NS - 8:NS - 4, :].rearrange("p s n -> p (s n)").rearrange("p (c n) -> p c n", c=DC)
        w2r0 = scores[:, NS - 4:NS, :].rearrange("p s n -> p (s n)").rearrange("p (c n) -> p c n", c=HC)
        in_w1 = [sem(f"in_w1{p}") for p in range(2)]
        in_w2 = [sem(f"in_w2{p}") for p in range(2)]

        def keep_warm(pe, bank, n):
            for _ in range(n):
                pe.matmul(bank[:, 0:P], ident[:], ident[:], start=True, stop=True)

        with ExitStack() as ctx:
            def sb(name, shape, dt):
                return ctx.enter_context(nc.sbuf_tensor(name, shape, dt))

            ps_s = [ctx.enter_context(nc.psum_tensor(f"ps_s{k}", [P, CH], F32)) for k in range(2)]
            ps_t = [ctx.enter_context(nc.psum_tensor(f"ps_t{k}", [P, CH], F32)) for k in range(2)]
            ps_o = [ctx.enter_context(nc.psum_tensor(f"ps_o{k}", [P, CH], F32)) for k in range(2)]
            ps_m = [ctx.enter_context(nc.psum_tensor(f"ps_m{k}", [P, CH], F32)) for k in range(2)]

            xT = [sb(f"xT{k}", [P, DC, S], F32R) for k in "hl"]
            V = [sb(f"V{k}", [P, NT, D], F32R) for k in "hl"]
            QT = [[sb(f"QT{p}{k}", [P, DC, 2 * P], F32R) for k in "hl"] for p in range(2)]
            PT = [[sb(f"PT{p}{k}", [P, CH], F32R) for k in "hl"] for p in range(2)]
            xn = [sb(f"xn{p}", [P, 2, D], F32) for p in range(2)]
            xres = [sb(f"xres{p}", [P, D], F32) for p in range(2)]
            x2 = [sb(f"x2{p}", [P, D], F32) for p in range(2)]
            xn2 = sb("xn2", [P, 2, D], F32)
            x2T = [sb(f"x2T{k}", [P, DC, 2 * P], F32R) for k in "hl"]
            trow = sb("trow", [P, 2, K2, ROW], F32)
            Mw = [sb(f"Mw{k}", [P, DC, D], F32R) for k in "hl"]
            Vws = [sb(f"Vw{k}", [P, DC, D], F32R) for k in "hl"]
            Wi = [sb(f"Wi{k}", [P, DC, GW], F32R) for k in "hl"]
            pad = sb("pad", [P, ROW], F32)
            causal = sb("causal", [P, CH], F32)
            bin_row = sb("bin_row", [P, D], F32)
            bin_col = sb("bin_col", [P, DC], F32)
            wg = sb("wg", [P, DC, E], F32)
            gate_bias = sb("gate_bias", [P, E], F32)
            bgate = sb("bgate", [P, E], F32)
            before = sb("before", [P, P], BF16)
            ones = sb("ones", [P, P], BF16)
            earlier = sb("earlier", [P, E, E], F32)
            target_i = sb("target_i", [P, NT, K2], I32)
            target = sb("target", [P, NT, K2], F32)
            base_i = sb("base_i", [P, E], I32)
            base = sb("base", [P, E], F32)
            tau_i = sb("tau_i", [P, NTILES], I32)
            tau = sb("tau", [P, NTILES], F32)
            mxs = sb("mxs", [P, NT, NCH], F32)
            negm = sb("negm", [P, NT], F32)
            lsum = sb("lsum", [P, NT, NCH], F32)
            rden = sb("rden", [P, 2], F32)
            stats = [sb(f"stats{k}", [P, 2, 6], F32) for k in range(2)]
            mv = [sb(f"mv{k}", [P, 2, 2], F32) for k in range(2)]
            nw = [sb(f"nw{k}", [P, 4, 2], F32) for k in range(2)]
            lg = sb("lg", [P, 2, E], F32)
            cmp = sb("cmp", [P, 2, 2, E, E], F32)
            rank = sb("rank", [P, 2, E], F32)
            pick = [sb(f"pick{k}", [P, 2, E], F32) for k in range(K2)]
            prod = sb("prod", [P, K2, 2, E], F32)
            lk = sb("lk", [P, K2, 2], F32)
            gd = sb("gd", [P, 2], F32)
            ge = sb("ge", [P, 2], F32)
            gs = sb("gs", [P, 2], F32)
            gr = sb("gr", [P, 2], F32)
            sel = sb("sel", [P, 2, E], BF16)
            cnt = sb("cnt", [P, E], F32)
            pos = sb("pos", [P, 2, E], F32)
            posf = sb("posf", [P, 2, K2], F32)
            slot = sb("slot", [P, NT, K2], U32)
            tabe = sb("tabe", [1, 4, E], F32)
            tabj = sb("tabj", [1, E, E], F32)
            base255 = sb("base255", [P, E], F32)
            tabi = sb("tabi", [1, E], I32)
            f32 = lambda ap: ap.bitcast(F32)

            wraw = [scores[:, NS - 1 - k, :].rearrange("p (c n) -> p c n", c=DC) for k in (3, 2, 0, 4)]
            wTr = [scores[:, NS - 1 - k, :].rearrange("p (c n) -> p c n", c=DC) for k in (5, 6, 1)]

            bin_wide = scores[:, NS - 3, 0:DC * P].rearrange("p (c n) -> p c n", c=DC)
            flat = scores[0:1, :, :].rearrange("p s n -> p (s n)")
            oneh = flat[:, 0:2 * NTILES * E].rearrange("p (k t e) -> p k t e", k=2, e=E)
            tabf = flat[:, 2 * NTILES * E:2 * NTILES * E + 4 * NTILES].rearrange("p (k t) -> p k t", k=4)
            assert 2 * NTILES * E + 4 * NTILES <= (NS - 8) * CH

            w_in = sem("w_in")
            qk_w_in = sem("qk_w_in")
            v_w_in = sem("v_w_in")
            x_ld = [sem(f"x_ld{p}") for p in range(2)]
            res_ld = [sem(f"res_ld{p}") for p in range(2)]
            consts = sem("consts")
            vchain = sem("vchain")
            pchain = sem("pchain")
            var_ready = [sem(f"var_ready{k}") for k in (1, 2)]
            log_done = [sem(f"log_done{k}") for k in (1, 2)]
            rstd_guess = [sem(f"rstd_guess{k}") for k in (1, 2)]
            ln_done = sem("ln_done")
            ln2_done = sem("ln2_done")
            wcast = sem("wcast")
            wdone = sem("wdone")
            vw_lo = sem("vw_lo")
            misc_full = sem("misc_full")
            misc_hi = sem("misc_hi")
            misc_done = sem("misc_done")
            scores_full = sem("scores_full")
            scores_out = sem("scores_out")
            max_ready = sem("max_ready")
            exp_done = sem("exp_done")
            pt_full = sem("pt_full")
            pt_hi = sem("pt_hi")
            pt_lo = sem("pt_lo")
            pv_done = sem("pv_done")
            fin_done = sem("fin_done")
            x2_stored = [sem(f"x2_stored{p}") for p in range(2)]
            x2_ld = sem("x2_ld")
            gate_diff = sem("gate_diff")
            gate_exp = sem("gate_exp")
            sel_ready = sem("sel_ready")
            slots_ready = sem("slots_ready")
            t_ready = sem("t_ready")
            scattered = sem("scattered")
            tables = sem("tables")
            counted = sem("counted")
            padded = sem("padded")
            block = ctx.enter_context(nc.Block())

            N_W = 6

            pad2 = pad[:].unsqueeze(1).to_broadcast([P, 2, ROW])

            def padding(eng, e):
                r = eng.snap(eng.value_load(pad_row[0:1, e:e + 1], min_val=0, max_val=E * REGION - TS))
                eng.dma_start(xs[bass.ds(r, TS), :].rearrange("(p a) d -> p a d", a=2), pad2).then_inc(padded, 16)

            @block.sync
            def _(sp):
                def load_x(h):
                    sp.dma_start(xn[h % 2][:], x[h * 2 * P:(h + 1) * 2 * P, :].rearrange(
                        "(t p) d -> p t d", p=P)).then_inc(x_ld[h % 2], 16)

                load_x(0)
                for k, w, arrived in ((0, Qw, qk_w_in), (1, Kw, qk_w_in), (3, Vw, v_w_in), (2, W_in, w_in)):
                    sp.dma_start(wraw[k], w.rearrange("(c p) n -> p c n", p=P)).then_inc(arrived, 16)
                sp.dma_start(wg[:], W_gate.rearrange("(c p) n -> p c n", p=P)).then_inc(w_in, 16)
                sp.dma_start(bin_row[:], rows_bcast(b_in, P)).then_inc(w_in, 16)
                sp.dma_start(bgate[:], rows_bcast(b_gate, P)).then_inc(w_in, 16)
                for c in range(DC):
                    sp.dma_start(bin_col[:, c:c + 1],
                                 b_in[c * P:(c + 1) * P].rearrange("(p a) -> p a", a=1)).then_inc(w_in, 16)
                for h in range(1, 2):
                    load_x(h)
                for it in plan:
                    if it[0] == "xT" and it[1] + 2 < NH:
                        sp.wait_ge(misc_full, job[it] + 1)
                        load_x(it[1] + 2)
                    elif it[0] == "mx":
                        i = it[1]
                        if i >= 2:
                            sp.wait_ge(fin_done, i - 1)
                        sp.dma_start(xres[i % 2][:], x[i * P:(i + 1) * P, :]).then_inc(res_ld[i % 2], 16)
                    elif it[0] == "fin":
                        i = it[1]
                        sp.wait_ge(fin_done, i + 1)
                        sp.dma_start(x2d[i * P:(i + 1) * P, :], x2[i % 2][:]).then_inc(x2_stored[i % 2], 16)
                    elif it[0] == "ld2" and it[1] < NH - 1:
                        h = it[1]
                        for p in range(2):
                            sp.wait_ge(x2_stored[p], 16 * (h + 1))
                        if h >= 1:
                            sp.wait_ge(misc_full, job[("fT", h - 1)] + 1)
                        sp.dma_start(xn2[:], x2d[h * 2 * P:(h + 1) * 2 * P, :].rearrange(
                            "(t p) d -> p t d", p=P)).then_inc(x2_ld, 16)
                sp.wait_ge(pt_full, chunk0[NT])
                sp.dma_start(w1r0, W1[0].rearrange("(c p) n -> p c n", p=P)).then_inc(in_w1[0], 16)
                sp.dma_start(w2r0, W2[0].rearrange("(p c) n -> p c n", c=HC)).then_inc(in_w2[0], 16)
                sp.dma_start(xs[E * REGION:E * REGION + TS, :].rearrange("(p a) d -> p a d", a=2),
                             pad2).then_inc(padded, 16)
                sp.wait_ge(counted, 1)
                for e in range(E // 2):
                    padding(sp, e)
                for p in range(2):
                    sp.wait_ge(x2_stored[p], 16 * NH)
                sp.wait_ge(padded, 16 * (E + 1))

            @block.gpsimd
            def _(pool):
                done = [0]

                def link(ins):
                    done[0] += 1
                    ins.then_inc(pchain, 1)
                    pool.wait_ge(pchain, done[0])

                link(pool.memset(ident[:], 0.0))
                pool.affine_select(out=ident[:], in_=ident[:], compare_op=ALU.not_equal, fill=1.0, base=0,
                                   pattern=[[-1, P]], channel_multiplier=1).then_inc(consts, 1)
                link(pool.memset(causal[:], 0.0))
                pool.affine_select(out=causal[:, CH - P:], in_=causal[:, CH - P:], compare_op=ALU.is_ge, fill=NEG,
                                   base=0, pattern=[[-1, P]], channel_multiplier=1).then_inc(consts, 1)
                link(pool.memset(before[:], 0.0))
                pool.affine_select(out=before[:], in_=before[:], compare_op=ALU.is_ge, fill=1.0, base=0,
                                   pattern=[[-1, P]], channel_multiplier=1).then_inc(consts, 1)
                pool.memset(ones[:], 1.0).then_inc(consts, 1)
                link(pool.memset(earlier[:], 0.0))
                pool.affine_select(out=earlier[:], in_=earlier[:], compare_op=ALU.is_ge, fill=1.0, base=0,
                                   pattern=[[-1, E], [1, E]], channel_multiplier=0).then_inc(consts, 1)
                pool.iota(target_i[:], pattern=[[2 * P, NT], [1, K2]], base=0,
                          channel_multiplier=2).then_inc(consts, 1)
                pool.iota(base_i[:], pattern=[[REGION, E]], base=0, channel_multiplier=0).then_inc(consts, 1)
                pool.iota(tau_i[:], pattern=[[1, NTILES]], base=0, channel_multiplier=0).then_inc(consts, 1)
                link(pool.memset(pad[:], 0.0))
                pool.memset(pad[:, D:ROW], NOWHERE).then_inc(consts, 1)
                for it in plan:
                    if it[0] == "route" and it[2] == 0:
                        h = it[1]
                        pool.wait_ge(misc_done, job[("t", h, 1)] + 1)
                        for s in range(2):
                            pool.tensor_copy(trow[:, s, 1, 0:D], trow[:, s, 0, 0:D]).then_inc(t_ready, 1)
                        pool.wait_ge(wdone, 1)
                        pool.tensor_copy(trow[:, :, :, D], target[:, 2 * h:2 * h + 2, :]).then_inc(t_ready, 1)
                    elif it[0] == "place" and it[2] == 1:
                        h = it[1]
                        pool.wait_ge(slots_ready, h + 1)
                        pool.wait_ge(t_ready, 3 * (h + 1))
                        for s in range(2):
                            for k in range(K2):
                                pool.indirect_dma_start(
                                    xs, bass.IndirectOffsetOnAxis(ap=slot[:, 2 * h + s, k:k + 1], axis=0),
                                    trow[:, s, k, :], None, bounds_check=E * REGION - 1).then_inc(scattered, 16)
                pool.wait_ge(scattered, 16 * 2 * K2 * NH)

            @block.scalar
            def _(act):
                act.preload_act_table_set("natural_log_exp_and_others")

                def hi(it, dst):
                    act.wait_ge(misc_full, job[it] + 1)
                    w = dst.free_size()
                    src = ps_m[job[it] % 2][:, 0:w]
                    if len(dst.shape) == 3:
                        src = src.rearrange("p (c n) -> p c n", c=dst.shape[1])
                    nc.scalar.copy(dst, src).then_inc(misc_hi, 1)

                for it in plan:
                    if it[0] == "Vw":
                        act.wait_ge(v_w_in, 16)
                        nc.scalar.copy(Vws[0][:], wraw[3]).then_inc(wcast, 1)
                    elif it[0] == "Wi":
                        act.wait_ge(w_in, 16 * N_W)
                        nc.scalar.copy(Wi[0][:, :, 0:D], wraw[2]).then_inc(wcast, 1)
                    elif it[0] == "M":
                        hi(it, Mw[0][:])
                    elif it[0] == "xT":
                        hi(it, xT[0][:, :, it[1] * 2 * P:(it[1] + 1) * 2 * P])
                    elif it[0] == "qm":
                        hi(it, QT[it[1] % 2][0][:])
                    elif it[0] == "v":
                        hi(it, V[0][:, 2 * it[1]:2 * it[1] + 2, :])
                    elif it[0] == "fT":
                        hi(it, x2T[0][:])
                    elif it[0] == "ex":
                        _, i, c = it
                        g = chunk0[i] + c
                        w, _w = width(i, c)
                        act.wait_ge(max_ready, i + 1)
                        p = scores[:, g % NS, 0:w]
                        nc.scalar.activation(p, p, ACT.Exp, bias=negm[:, i:i + 1], scale=SCALE,
                                             accum_out=lsum[:, i, c:c + 1]).then_inc(exp_done, 1)
                    elif it[0] == "tp":
                        _, i, c = it
                        g = chunk0[i] + c
                        w, _w = width(i, c)
                        act.wait_ge(pt_full, g + 1)
                        if g >= 2:
                            act.wait_ge(pv_done, g - 1)
                        nc.scalar.copy(PT[g % 2][0][:, 0:w], ps_t[g % 2][:, 0:w]).then_inc(pt_hi, 1)
                    elif it[0] in ("ln1", "ln2") and it[2] == 1:
                        k = int(it[0] == "ln2")
                        act.wait_ge(var_ready[k], it[1] + 1)
                        nc.scalar.activation(nw[k][:, 1, :], nw[k][:, 0, :], ACT.Ln).then_inc(log_done[k], 1)
                        act.wait_ge(log_done[k], it[1] + 1)
                        nc.scalar.activation(nw[k][:, 2, :], nw[k][:, 1, :], ACT.Exp,
                                             scale=-0.5).then_inc(rstd_guess[k], 1)
                    elif it[0] == "route" and it[2] == 2:
                        act.wait_ge(gate_diff, it[1] + 1)
                        nc.scalar.activation(ge[:], gd[:], ACT.Exp).then_inc(gate_exp, 1)
                act.wait_ge(counted, 1)
                for e in range(E // 2, E):
                    padding(nc.scalar, e)

            @block.tensor
            def _(pe):
                def bank(it):
                    n = job[it]
                    if n >= 2:
                        pe.wait_ge(misc_done, n - 1)
                    return ps_m[n % 2]

                pe.wait_ge(consts, 1)
                keep_warm(pe, ps_o[0], 10)
                pe.wait_ge(consts, 9)
                for it in plan:
                    kind = it[0]
                    if kind == "wT":
                        if it[1] == 0:
                            pe.wait_ge(qk_w_in, 16 * 2)
                        elif it[1] == 2:
                            pe.wait_ge(w_in, 16 * N_W)
                        ps = bank(it)
                        for ce in range(DC):
                            for cd in range(DC):
                                at = ce * D + cd * P
                                last = pe.transpose(ps[:, at:at + P], wraw[it[1]][:, cd, ce * P:(ce + 1) * P],
                                                    ident[:])
                        last.then_inc(misc_full, 1)
                    elif kind == "M":
                        keep_warm(pe, ps_o[0], 4)
                        pe.wait_ge(misc_done, job[("wT", 1)] + 1)
                        ps = bank(it)
                        for cd in range(DC):
                            for ce in range(DC):
                                last = pe.matmul(ps[:, cd * D:(cd + 1) * D], wTr[0][:, ce, cd * P:(cd + 1) * P],
                                                 wTr[1][:, ce, :], start=(ce == 0), stop=(ce == DC - 1))
                        last.then_inc(misc_full, 1)
                    elif kind == "G":
                        pe.wait_ge(misc_done, job[("wT", 2)] + 1)
                        ps = bank(it)
                        pe.wait_ge(wdone, 3)
                        for cd in range(DC + 1):
                            for ce in range(DC):
                                w = wTr[2][:, ce, cd * P:(cd + 1) * P] if cd < DC else bin_wide[:, ce, :]
                                last = pe.matmul(ps[:, cd * E:(cd + 1) * E], w, wg[:, ce, :],
                                                 start=(ce == 0), stop=(ce == DC - 1))
                        last.then_inc(misc_full, 1)
                    elif kind in ("xT", "fT"):
                        h = it[1]
                        if kind == "xT":
                            pe.wait_ge(ln_done, h + 1)
                        else:
                            pe.wait_ge(ln2_done, h + 1)
                        src = xn[h % 2] if kind == "xT" else xn2
                        ps = bank(it)
                        for s in range(2):
                            for c in range(DC):
                                at = c * 2 * P + s * P
                                last = pe.transpose(ps[:, at:at + P], src[:, s, c * P:(c + 1) * P], ident[:])
                        last.then_inc(misc_full, 1)
                    elif kind == "qm":
                        h = it[1]
                        pe.wait_ge(misc_done, max(job[("xT", h)], job[("M", 0)]) + 1)
                        ps = bank(it)
                        for c2 in range(DC):
                            for c1 in range(DC):
                                last = mm3(pe, ps[:, c2 * D:(c2 + 1) * D],
                                           [m[:, c1, c2 * P:(c2 + 1) * P] for m in Mw],
                                           [t[:, c1, h * 2 * P:(h + 1) * 2 * P] for t in xT],
                                           c1 == 0, c1 == DC - 1)
                        last.then_inc(misc_full, 1)
                    elif kind == "v":
                        h = it[1]
                        pe.wait_ge(vw_lo, 1)
                        ps = bank(it)
                        for s in range(2):
                            for c in range(DC):
                                at = (2 * h + s) * P
                                last = mm3(pe, ps[:, s * D:(s + 1) * D], [t[:, c, at:at + P] for t in xT],
                                           [w[:, c, :] for w in Vws], c == 0, c == DC - 1)
                        last.then_inc(misc_full, 1)
                    elif kind == "t":
                        _, h, s = it
                        pe.wait_ge(misc_done, job[("fT", h)] + 1)
                        pe.wait_ge(wdone, 5)
                        ps = bank(it)
                        for c in range(DC):
                            last = mm3(pe, ps[:, 0:GW], [t[:, c, s * P:(s + 1) * P] for t in x2T],
                                       [w[:, c, :] for w in Wi], c == 0, c == DC - 1)
                        last.then_inc(misc_full, 1)
                    elif kind == "pre":
                        h = it[1]
                        pe.wait_ge(sel_ready, h + 1)
                        ps = bank(it)
                        s2 = sel[:].rearrange("p t e -> p (t e)")
                        pe.matmul(ps[:, 0:2 * E], before[:], s2, start=True, stop=True)
                        pe.matmul(ps[:, 2 * E:4 * E], ones[:], s2, start=True, stop=True).then_inc(misc_full, 1)
                    elif kind == "qk":
                        _, i, c = it
                        g = chunk0[i] + c
                        w, wide = width(i, c)
                        if c == 0:
                            pe.wait_ge(misc_done, job[("qm", i // 2)] + 1)
                        if g >= 2:
                            pe.wait_ge(scores_out, g - 1)
                        at = (i % 2) * P
                        for d in range(DC):
                            last = mm3(pe, ps_s[g % 2][:, 0:wide], [q[:, d, at:at + P] for q in QT[i // 2 % 2]],
                                       [t[:, d, c * CH:c * CH + wide] for t in xT], d == 0, d == DC - 1)
                        last.then_inc(scores_full, 1)
                    elif kind == "tp":
                        _, i, c = it
                        g = chunk0[i] + c
                        w, _w = width(i, c)
                        pe.wait_ge(exp_done, g + 1)
                        if g >= 2:
                            pe.wait_ge(pt_lo, g - 1)
                        for k in range(w // P):
                            last = pe.transpose(ps_t[g % 2][:, k * P:(k + 1) * P],
                                                scores[:, g % NS, k * P:(k + 1) * P], ident[:])
                        last.then_inc(pt_full, 1)
                    elif kind == "pv":
                        _, i, c = it
                        g = chunk0[i] + c
                        w, _w = width(i, c)
                        pe.wait_ge(pt_lo, g + 1)
                        if c == 0:
                            pe.wait_ge(misc_done, job[("v", i // 2)] + 1)
                            if i >= 2:
                                pe.wait_ge(fin_done, i - 1)
                        for k in range(w // P):
                            kt = c * 4 + k
                            last = mm3(pe, ps_o[i % 2][:, 0:D], [p[:, k * P:(k + 1) * P] for p in PT[g % 2]],
                                       [v[:, kt, :] for v in V], kt == 0, kt == i)
                        last.then_inc(pv_done, 1)
                keep_warm(pe, ps_o[0], 38)

            @block.vector
            def _(dve):
                done = [0]

                def link(ins):
                    done[0] += 1
                    ins.then_inc(vchain, 1)
                    dve.wait_ge(vchain, done[0])

                def layernorm(k, h, src, dst, ready, piece):
                    v, _log, y, a = (nw[k][:, j, :] for j in range(4))
                    if piece == 0:
                        for s in range(2):
                            last = dve.bn_stats(stats[k][:, s, :], src[s])
                        link(last)
                        for s in range(2):
                            last = dve.bn_aggr(mv[k][:, s, :], stats[k][:, s, :])
                        link(last)
                        dve.tensor_scalar(v, mv[k][:, :, 1], EPS, None, ALU.add).then_inc(var_ready[k], 1)
                    elif piece == 2:
                        dve.wait_ge(rstd_guess[k], h + 1)
                        link(dve.scalar_tensor_tensor(a, y, -0.5, y, ALU.mult, ALU.mult))
                        link(dve.tensor_tensor(a, a, v, ALU.mult))
                        link(dve.scalar_tensor_tensor(y, a, 1.5, y, ALU.add, ALU.mult))
                        for s in range(2):
                            last = dve.tensor_scalar(dst[:, s, :], src[s], mv[k][:, s, 0:1], y[:, s:s + 1],
                                                     ALU.subtract, ALU.mult)
                        last.then_inc(ready, 1)

                def lo(it, dst, hi_part):
                    dve.wait_ge(misc_hi, hijob[it] + 1)
                    src = ps_m[job[it] % 2][:, 0:dst.free_size()].rearrange("p (c n) -> p c n", c=dst.shape[1])
                    dve.tensor_tensor(dst, src, f32(hi_part), ALU.subtract).then_inc(misc_done, 1)

                dve.wait_ge(consts, 9)
                dve.tensor_copy(target[:], target_i[:]).then_inc(wdone, 1)
                dve.tensor_copy(tau[:], tau_i[:])
                dve.tensor_scalar(base255[:], base_i[:], -float(TS - 1), None, ALU.add)
                dve.tensor_copy(base[:], base_i[:]).then_inc(wdone, 1)
                dve.wait_ge(wdone, 2)
                link(dve.tensor_copy(cnt[:], base[:]))
                for it in plan:
                    kind = it[0]
                    if kind == "Vw":
                        dve.wait_ge(wcast, 1)
                        dve.tensor_tensor(Vws[1][:], wraw[3], f32(Vws[0][:]), ALU.subtract).then_inc(vw_lo, 1)
                    elif kind == "Wi":
                        dve.wait_ge(w_in, 16 * N_W)
                        for c in range(DC):
                            last = dve.tensor_copy(bin_wide[:, c, :], bin_col[:, c:c + 1].to_broadcast([P, P]))
                        last.then_inc(wdone, 1)
                        dve.wait_ge(wcast, 2)
                        dve.tensor_tensor(Wi[1][:, :, 0:D], wraw[2], f32(Wi[0][:, :, 0:D]),
                                          ALU.subtract).then_inc(wdone, 1)
                    elif kind == "wT":
                        dve.wait_ge(misc_full, job[it] + 1)
                        dve.tensor_copy(wTr[it[1]], ps_m[job[it] % 2][:].rearrange("p (c n) -> p c n", c=DC))\
                           .then_inc(misc_done, 1)
                    elif kind == "M":
                        lo(it, Mw[1][:], Mw[0][:])
                    elif kind == "G":
                        dve.wait_ge(misc_full, job[it] + 1)
                        ps = ps_m[job[it] % 2]
                        g2 = ps[:, 0:DC * E].rearrange("p (c e) -> p c e", c=DC)
                        link(dve.tensor_copy(Wi[0][:, :, D:GW], g2))
                        dve.tensor_tensor(Wi[1][:, :, D:GW], g2, f32(Wi[0][:, :, D:GW]),
                                          ALU.subtract).then_inc(wdone, 1)
                        dve.tensor_tensor(gate_bias[:], ps[:, DC * E:(DC + 1) * E], bgate[:],
                                          ALU.add).then_inc(misc_done, 1)
                        dve.wait_ge(misc_done, job[it] + 1)
                    elif kind == "ln1":
                        h = it[1]
                        dve.wait_ge(x_ld[h % 2], 16 * (h // 2 + 1))
                        layernorm(0, h, [xn[h % 2][:, s, :] for s in range(2)], xn[h % 2], ln_done, it[2])
                    elif kind == "ln2":
                        h = it[1]
                        if h < NH - 1:
                            dve.wait_ge(x2_ld, 16 * (h + 1))
                            layernorm(1, h, [xn2[:, s, :] for s in range(2)], xn2, ln2_done, it[2])
                        else:
                            if it[2] == 0:
                                dve.wait_ge(fin_done, NT)
                            elif it[2] == 2:
                                dve.wait_ge(misc_full, job[("fT", h - 1)] + 1)
                            layernorm(1, h, [x2[s][:] for s in range(2)], xn2, ln2_done, it[2])
                    elif kind == "xT":
                        at = slice(it[1] * 2 * P, (it[1] + 1) * 2 * P)
                        lo(it, xT[1][:, :, at], xT[0][:, :, at])
                    elif kind == "qm":
                        q = QT[it[1] % 2]
                        lo(it, q[1][:], q[0][:])
                    elif kind == "v":
                        at = slice(2 * it[1], 2 * it[1] + 2)
                        lo(it, V[1][:, at, :], V[0][:, at, :])
                    elif kind == "fT":
                        lo(it, x2T[1][:], x2T[0][:])
                    elif kind == "qk":
                        _, i, c = it
                        g = chunk0[i] + c
                        w, _w = width(i, c)
                        dve.wait_ge(scores_full, g + 1)
                        if g >= NS:
                            dve.wait_ge(pt_full, g - NS + 1)
                        diag = c == i // 4
                        mask = causal[:, CH - w:] if diag else causal[:, 0:1].to_broadcast([P, w])
                        dve.tensor_tensor_reduce(scores[:, g % NS, 0:w], ps_s[g % 2][:, 0:w], mask, 1.0, NEG,
                                                 ALU.add, ALU.max, mxs[:, i, c:c + 1]).then_inc(scores_out, 1)
                    elif kind == "mx":
                        i = it[1]
                        dve.wait_ge(scores_out, chunk0[i + 1])
                        link(dve.tensor_reduce(negm[:, i:i + 1], mxs[:, i, 0:i // 4 + 1], AX.X, ALU.max))
                        dve.tensor_scalar(negm[:, i:i + 1], negm[:, i:i + 1], -SCALE, None,
                                          ALU.mult).then_inc(max_ready, 1)
                    elif kind == "tp":
                        _, i, c = it
                        g = chunk0[i] + c
                        w, _w = width(i, c)
                        dve.wait_ge(pt_hi, g + 1)
                        dve.tensor_tensor(PT[g % 2][1][:, 0:w], ps_t[g % 2][:, 0:w],
                                          f32(PT[g % 2][0][:, 0:w]), ALU.subtract).then_inc(pt_lo, 1)
                    elif kind == "fin":
                        i = it[1]
                        dve.wait_ge(pv_done, chunk0[i + 1])
                        link(dve.tensor_reduce(rden[:, 0:1], lsum[:, i, 0:i // 4 + 1], AX.X, ALU.add))
                        link(dve.reciprocal(rden[:, 1:2], rden[:, 0:1]))
                        dve.wait_ge(res_ld[i % 2], 16 * (i // 2 + 1))
                        if i >= 2:
                            dve.wait_ge(x2_stored[i % 2], 16 * (i // 2))
                        dve.scalar_tensor_tensor(x2[i % 2][:], ps_o[i % 2][:, 0:D], rden[:, 1:2],
                                                 xres[i % 2][:], ALU.mult, ALU.add).then_inc(fin_done, 1)
                    elif kind == "t":
                        _, h, s = it
                        if s == 0 and h >= 1:
                            dve.wait_ge(scattered, 16 * 2 * K2 * h)
                        dve.wait_ge(misc_full, job[it] + 1)
                        ps = ps_m[job[it] % 2]
                        dve.tensor_tensor(trow[:, s, 0, 0:D], ps[:, 0:D], bin_row[:], ALU.add)
                        dve.tensor_tensor(lg[:, s, :], ps[:, D:GW], gate_bias[:], ALU.add)\
                           .then_inc(misc_done, 1)
                    elif kind == "route" and it[2] == 0:
                        dve.wait_ge(misc_done, job[("t", it[1], 1)] + 1)
                        lj = lg[:].unsqueeze(2).to_broadcast([P, 2, E, E])
                        le = lg[:].unsqueeze(3).to_broadcast([P, 2, E, E])
                        link(dve.tensor_tensor(cmp[:, 1], lj, le, ALU.is_equal))
                        dve.tensor_tensor(cmp[:, 0], lj, le, ALU.is_gt)
                        link(dve.tensor_tensor(cmp[:, 1], cmp[:, 1],
                                               earlier[:].unsqueeze(1).to_broadcast([P, 2, E, E]), ALU.mult))
                        link(dve.tensor_tensor(cmp[:, 0], cmp[:, 0], cmp[:, 1], ALU.add))
                    elif kind == "route" and it[2] == 1:
                        link(dve.tensor_reduce(rank[:], cmp[:, 0], AX.X, ALU.add))
                        dve.tensor_scalar(sel[:], rank[:], float(K2), None, ALU.is_lt).then_inc(sel_ready, 1)
                        for k in range(K2):
                            last = dve.tensor_scalar(pick[k][:], rank[:], float(k), None, ALU.is_equal)
                        link(last)
                    elif kind == "route":
                        for k in range(K2):
                            last = dve.tensor_tensor(prod[:, k], pick[k][:], lg[:], ALU.mult)
                        link(last)
                        link(dve.tensor_reduce(lk[:], prod[:], AX.X, ALU.add))
                        dve.tensor_tensor(gd[:], lk[:, 1, :], lk[:, 0, :], ALU.subtract).then_inc(gate_diff, 1)
                    elif kind == "pre":
                        dve.wait_ge(misc_full, job[it] + 1)
                        ps = ps_m[job[it] % 2]
                        dve.tensor_tensor(pos[:, 0, :], ps[:, 0:E], cnt[:], ALU.add)
                        link(dve.tensor_tensor(cnt[:], ps[:, 2 * E:3 * E], cnt[:], ALU.add))
                        dve.tensor_tensor(pos[:, 1, :], ps[:, E:2 * E], cnt[:], ALU.add)
                        dve.tensor_tensor(cnt[:], ps[:, 3 * E:4 * E], cnt[:], ALU.add).then_inc(misc_done, 1)
                        dve.wait_ge(misc_done, job[it] + 1)
                        if it[1] == NH - 1:
                            dve.tensor_copy(pad_row[:], cnt[0:1, :]).then_inc(counted, 1)
                    elif kind == "place" and it[2] == 0:
                        for k in range(K2):
                            last = dve.tensor_tensor(prod[:, k], pick[k][:], pos[:], ALU.mult)
                        link(last)
                    elif kind == "place" and it[2] == 1:
                        h = it[1]
                        for k in range(K2):
                            last = dve.tensor_reduce(posf[:, :, k], prod[:, k], AX.X, ALU.add)
                        link(last)
                        dve.tensor_copy(slot[:, 2 * h:2 * h + 2, :], posf[:]).then_inc(slots_ready, 1)
                    elif kind == "place":
                        h = it[1]
                        dve.wait_ge(gate_exp, h + 1)
                        link(dve.tensor_scalar(gs[:], ge[:], 1.0, None, ALU.add))
                        link(dve.reciprocal(gr[:], gs[:]))
                        dve.tensor_copy(route_w[:, 2 * h:2 * h + 2, 0], gr[:])
                        link(dve.tensor_tensor(route_w[:, 2 * h:2 * h + 2, 1], gr[:], ge[:], ALU.mult))

                rowf, expf, part = (tabf[:, k, :] for k in range(3))
                tiles, excl, incl, delta = (tabe[:, k, :] for k in range(4))
                t0 = tau[0:1, :]
                link(dve.tensor_tensor(tabi[:], cnt[0:1, :], base255[0:1, :], ALU.subtract))
                link(dve.tensor_scalar(tabi[:], tabi[:], TS.bit_length() - 1, None, ALU.logical_shift_right))
                link(dve.tensor_scalar(tiles, tabi[:], 1.0, None, ALU.max))
                link(dve.tensor_tensor(tabj[:], earlier[0:1], tiles.unsqueeze(1).to_broadcast([1, E, E]), ALU.mult))
                link(dve.tensor_reduce(excl, tabj[:], AX.X, ALU.add))
                dve.tensor_tensor(incl, excl, tiles, ALU.add)
                link(dve.scalar_tensor_tensor(delta, excl, -float(TS), base[0:1, :], ALU.mult, ALU.add))
                sh = [1, NTILES, E]
                tb = t0.unsqueeze(2).to_broadcast(sh)
                dve.tensor_tensor(oneh[:, 1], tb, excl.unsqueeze(1).to_broadcast(sh), ALU.is_ge)
                link(dve.tensor_tensor(oneh[:, 0], tb, incl.unsqueeze(1).to_broadcast(sh), ALU.is_ge))
                dve.tensor_reduce(expf, oneh[:, 0], AX.X, ALU.add)
                link(dve.tensor_tensor(oneh[:, 1], oneh[:, 1], oneh[:, 0], ALU.subtract))
                link(dve.tensor_tensor(oneh[:, 1], oneh[:, 1], delta.unsqueeze(1).to_broadcast(sh), ALU.mult))
                dve.tensor_scalar(tile_expert[:], expf, float(E - 1), None, ALU.min)
                link(dve.tensor_reduce(rowf, oneh[:, 1], AX.X, ALU.add))
                link(dve.scalar_tensor_tensor(rowf, t0, float(TS), rowf, ALU.mult, ALU.add))
                link(dve.scalar_tensor_tensor(part, oneh[:, 0, :, E - 1], float(E * REGION), rowf, ALU.mult, ALU.add))
                dve.tensor_scalar(tile_row[:], part, float(E * REGION), None, ALU.min).then_inc(tables, 1)
                dve.wait_ge(tables, 1)

        XG = 8
        xall = sbk("xall", [P, NT, D], F32)
        wor = sbk("wor", [P, DC, D], F32)
        wo = [sbk(f"wo{k}", [P, DC, D], F32R) for k in "hl"]
        bo = sbk("bo", [P, D], F32)
        wo_in = sem("wo_in")
        wo_hi = sem("wo_hi")
        xall_in = sem("xall_in")

        with ExitStack() as ctx:
            def sb(name, shape, dt):
                return ctx.enter_context(nc.sbuf_tensor(name, shape, dt))

            ps_x = ctx.enter_context(nc.psum_tensor("ps_x", [P, CH], F32))
            NHB = 3
            ps_h = [ctx.enter_context(nc.psum_tensor(f"ps_h{k}", [P, CH], F32)) for k in range(NHB)]
            ps_e = [[ctx.enter_context(nc.psum_tensor(f"ps_e{p}{s}", [P, CH], F32)) for s in range(2)]
                    for p in range(2)]
            HQ = HC // 2
            xr = [sb(f"xr{p}", [P, 2, ROW], F32) for p in range(2)]
            w1r = [w1r0, sb("w1r1", [P, DC, F], F32)[:]]
            w2r = [w2r0, sb("w2r1", [P, HC, D], F32)[:]]
            b1s = [sb(f"b1s{p}", [P, HC], F32) for p in range(2)]
            b2s = [sb(f"b2s{p}", [P, D], F32) for p in range(2)]
            w1 = [[sb(f"w1{p}{k}", [P, DC, HC, P], F32R) for k in "hl"] for p in range(2)]
            w2 = [[sb(f"w2{p}{k}", [P, HC, D], F32R) for k in "hl"] for p in range(2)]
            xrT = [sb(f"xrT{k}", [P, DC, TS], F32R) for k in "hl"]
            mid = sb("mid", [P, HC, TS], F32)
            midT = [sb(f"midT{k}", [P, HC, TS], F32R) for k in "hl"]
            esb = [sb(f"esb{p}", [P, 2, D], F32) for p in range(2)]
            eidx = [sb(f"eidx{p}", [P, 2], U32) for p in range(2)]
            f32 = lambda ap: ap.bitcast(F32)

            in_x = [sem(f"in_x{p}") for p in range(2)]
            in_b = [sem(f"in_b{p}") for p in range(2)]
            xt_full = sem("xt_full")
            xt_hi = sem("xt_hi")
            xt_lo = sem("xt_lo")
            w1_hi = sem("w1_hi")
            w1_lo = sem("w1_lo")
            w2_hi = sem("w2_hi")
            w2_lo = sem("w2_lo")
            hid_full = sem("hid_full")
            relu_done = sem("relu_done")
            mid_hi = sem("mid_hi")
            mid_lo = sem("mid_lo")
            h1_done = sem("h1_done")
            e_full = sem("e_full")
            e_out = sem("e_out")
            idx_done = sem("idx_done")
            e_stored = [sem(f"e_stored{p}") for p in range(2)]
            block = ctx.enter_context(nc.Block())

            def over_tiles(eng, body, first):
                n = (NTILES - first) // 2
                with eng.Fori(0, n) as j:
                    for k in range(2):
                        body(j * 2 + (first + k), (first + k) % 2)
                for t in range(first + 2 * n, NTILES):
                    body(t, t % 2)

            def half(t):
                return t // 2

            @block.sync
            def _(sp):
                def load(t, p, head):
                    r = sp.snap(sp.value_load(tile_row[0:1, bass.ds(t, 1)], min_val=0, max_val=E * REGION))
                    e = sp.snap(sp.value_load(tile_expert[0:1, bass.ds(t, 1)], min_val=0, max_val=E - 1))
                    if not head:
                        done = sp.snap(t - 1)
                        q1 = sp.snap(DC * (t - 1))
                        q2 = sp.snap(HQ * (t - 1))
                        sp.wait_ge(xt_full, done)
                        sp.wait_ge(idx_done, done)
                    sp.dma_start(xr[p][:], xs[bass.ds(r, TS), :].rearrange("(a q) d -> q a d", q=P))\
                      .then_inc(in_x[p], 16)
                    if not head:
                        sp.wait_ge(w1_lo, q1)
                    sp.dma_start(w1r[p], W1[bass.ds(e, 1), :, :].rearrange("a (c q) n -> q (a c) n", q=P))\
                      .then_inc(in_w1[p], 16)
                    if not head:
                        sp.wait_ge(w2_lo, q2)
                    sp.dma_start(w2r[p], W2[bass.ds(e, 1), :, :].rearrange("a (q c) n -> q (a c) n", c=HC))\
                      .then_inc(in_w2[p], 16)
                    if not head:
                        sp.wait_ge(e_out, done)
                    sp.dma_start(b1s[p][:], b1[bass.ds(e, 1), :].rearrange("a (q c) -> q (a c)", c=HC))\
                      .then_inc(in_b[p], 16)
                    sp.dma_start(b2s[p][:], b2[bass.ds(e, 1), :].partition_broadcast(P).rearrange(
                        "q a n -> q (a n)")).then_inc(in_b[p], 16)

                sp.dma_start(xr[0][:], xs[0:TS, :].rearrange("(a q) d -> q a d", q=P)).then_inc(in_x[0], 16)
                sp.dma_start(b1s[0][:], b1[0].rearrange("(q c) -> q c", c=HC)).then_inc(in_b[0], 16)
                sp.dma_start(b2s[0][:], rows_bcast(b2[0], P)).then_inc(in_b[0], 16)
                load(1, 1, True)
                over_tiles(sp, lambda t, p: load(t, p, False), 2)
                sp.dma_start(wor[:], W_out.rearrange("(c p) n -> p c n", p=P)).then_inc(wo_in, 16)
                sp.dma_start(bo[:], rows_bcast(b_out, P)).then_inc(wo_in, 16)
                for g in range(NT // XG):
                    sp.dma_start(xall[:, g * XG:(g + 1) * XG, :], x2d[g * XG * P:(g + 1) * XG * P, :].rearrange(
                        "(t p) d -> p t d", p=P)).then_inc(xall_in, 16)

            @block.gpsimd
            def _(pool):
                def store(t, p, head):
                    if not head:
                        pool.wait_ge(e_stored[p], 32 * half(t))
                    pool.wait_ge(in_x[p], 16 * (half(t) + 1))
                    pool.tensor_copy(eidx[p][:], xr[p][:, :, D]).then_inc(idx_done, 1)
                    pool.wait_ge(idx_done, t + 1)
                    pool.wait_ge(e_out, t + 1)
                    for s in range(2):
                        pool.indirect_dma_start(
                            yk, bass.IndirectOffsetOnAxis(ap=eidx[p][:, s:s + 1], axis=0), esb[p][:, s, :], None,
                            bounds_check=K2 * S - 1, oob_is_err=False).then_inc(e_stored[p], 16)

                for t in range(NTILES):
                    store(t, t % 2, t < 2)
                for p in range(2):
                    pool.wait_ge(e_stored[p], 32 * ((NTILES - p + 1) // 2))

            @block.scalar
            def _(act):
                def split_w1(t, p, c):
                    if c == 0:
                        act.wait_ge(in_w1[p], 16 * (half(t) + 1))
                    nc.scalar.copy(w1[p][0][:, c].rearrange("q h m -> q m h"),
                                   w1r[p][:, c, :].rearrange("q (m h) -> q m h", h=HC)).then_inc(w1_hi, 1)

                def split_w2(t, p, q):
                    if q == 0:
                        act.wait_ge(in_w2[p], 16 * (half(t) + 1))
                    nc.scalar.copy(w2[p][0][:, 2 * q:2 * q + 2, :], w2r[p][:, 2 * q:2 * q + 2, :]).then_inc(w2_hi, 1)

                def rows_hi(t):
                    act.wait_ge(xt_full, t + 1)
                    nc.scalar.copy(xrT[0][:], ps_x[:].rearrange("q (c n) -> q c n", c=DC)).then_inc(xt_hi, 1)

                def tile(t, p, last):
                    for q in range(HQ):
                        if q == 0:
                            act.wait_ge(in_b[p], 32 * (half(t) + 1))
                        act.wait_ge(hid_full, t * HQ + (q + 1))
                        for k in range(2):
                            h = 2 * q + k
                            r = nc.scalar.activation(mid[:, h, :], ps_h[q % 2][:, k * TS:(k + 1) * TS], ACT.Relu,
                                                     bias=b1s[p][:, h:h + 1])
                        r.then_inc(relu_done, 1)
                        if not last and q < DC:
                            split_w1(t + 1, 1 - p, q)
                    if not last:
                        rows_hi(t + 1)
                        for q in range(HQ):
                            split_w2(t + 1, 1 - p, q)

                for c in range(DC):
                    split_w1(0, 0, c)
                rows_hi(0)
                for q in range(HQ):
                    split_w2(0, 0, q)
                n = (NTILES - 1) // 2
                with act.Fori(0, n) as j:
                    for k in range(2):
                        tile(j * 2 + k, k, False)
                for t in range(2 * n, NTILES):
                    tile(t, t % 2, t == NTILES - 1)
                act.wait_ge(wo_in, 32)
                nc.scalar.copy(wo[0][:], wor[:]).then_inc(wo_hi, 1)

            @block.tensor
            def _(pe):
                def rows(t, p, head):
                    if not head:
                        pe.wait_ge(xt_lo, t)
                    pe.wait_ge(in_x[p], 16 * (half(t) + 1))
                    for s in range(2):
                        for c in range(DC):
                            at = c * TS + s * P
                            last = pe.transpose(ps_x[:, at:at + P], xr[p][:, s, c * P:(c + 1) * P], ident[:])
                    last.then_inc(xt_full, 1)

                def tile(t, p, first, head, last_tile):
                    for q in range(HQ):
                        if not first:
                            pe.wait_ge(relu_done, t * HQ + (q - 1))
                        elif q >= 2:
                            pe.wait_ge(relu_done, q - 1)
                        if q == 0:
                            pe.wait_ge(xt_lo, t + 1)
                            pe.wait_ge(w1_lo, DC * (t + 1))
                        for k in range(2):
                            h = 2 * q + k
                            for c in range(DC):
                                last = mm3(pe, ps_h[q % 2][:, k * TS:(k + 1) * TS], [w[:, c, h, :] for w in w1[p]],
                                           [x_[:, c, :] for x_ in xrT], c == 0, c == DC - 1)
                        last.then_inc(hid_full, 1)
                    if not last_tile:
                        rows(t + 1, 1 - p, False)
                    for q in range(HQ):
                        pe.wait_ge(mid_lo, t * HQ + (q + 1))
                        if q == 0:
                            pe.wait_ge(w2_lo, HQ * (t + 1))
                            if not head:
                                pe.wait_ge(e_out, t - 1)
                        for h in (2 * q, 2 * q + 1):
                            for s in range(2):
                                last = mm3(pe, ps_e[p][s][:, 0:D], [m[:, h, s * P:(s + 1) * P] for m in midT],
                                           [w[:, h, :] for w in w2[p]], h == 0, h == HC - 1)
                    last.then_inc(e_full, 1)

                keep_warm(pe, ps_e[0][0], 12)
                rows(0, 0, True)
                tile(0, 0, True, True, False)
                tile(1, 1, False, True, False)
                n = (NTILES - 3) // 2
                with pe.Fori(0, n) as j:
                    for k in range(2):
                        tile(j * 2 + (k + 2), k, False, False, False)
                for t in range(2 + 2 * n, NTILES):
                    tile(t, t % 2, False, False, t == NTILES - 1)
                keep_warm(pe, ps_x, 16)

            @block.vector
            def _(dve):
                def split_w1(t, p, c):
                    dve.wait_ge(w1_hi, DC * t + (c + 1))
                    dve.tensor_tensor(w1[p][1][:, c].rearrange("q h m -> q m h"),
                                      w1r[p][:, c, :].rearrange("q (m h) -> q m h", h=HC),
                                      f32(w1[p][0][:, c]).rearrange("q h m -> q m h"),
                                      ALU.subtract).then_inc(w1_lo, 1)

                def split_w2(t, p, q):
                    dve.wait_ge(w2_hi, HQ * t + (q + 1))
                    at = slice(2 * q, 2 * q + 2)
                    dve.tensor_tensor(w2[p][1][:, at, :], w2r[p][:, at, :], f32(w2[p][0][:, at, :]),
                                      ALU.subtract).then_inc(w2_lo, 1)

                def rows_lo(t):
                    dve.wait_ge(xt_hi, t + 1)
                    dve.tensor_tensor(xrT[1][:], ps_x[:].rearrange("q (c n) -> q c n", c=DC), f32(xrT[0][:]),
                                      ALU.subtract).then_inc(xt_lo, 1)

                def tile(t, p, head, last):
                    for q in range(HQ):
                        at = slice(2 * q, 2 * q + 2)
                        dve.wait_ge(relu_done, t * HQ + (q + 1))
                        dve.tensor_copy(midT[0][:, at, :], mid[:, at, :]).then_inc(mid_hi, 1)
                        dve.wait_ge(mid_hi, t * HQ + (q + 1))
                        dve.tensor_tensor(midT[1][:, at, :], mid[:, at, :], f32(midT[0][:, at, :]),
                                          ALU.subtract).then_inc(mid_lo, 1)
                        if not last and q < DC:
                            split_w1(t + 1, 1 - p, q)
                    if not last:
                        rows_lo(t + 1)
                        for q in range(HQ):
                            split_w2(t + 1, 1 - p, q)
                    if not head:
                        dve.wait_ge(e_stored[p], 32 * half(t))
                    dve.wait_ge(e_full, t + 1)
                    for s in range(2):
                        r = dve.tensor_tensor(esb[p][:, s, :], ps_e[p][s][:, 0:D], b2s[p][:], ALU.add)
                    r.then_inc(e_out, 1)

                for c in range(DC):
                    split_w1(0, 0, c)
                rows_lo(0)
                for q in range(HQ):
                    split_w2(0, 0, q)
                tile(0, 0, True, False)
                tile(1, 1, True, False)
                n = (NTILES - 3) // 2
                with dve.Fori(0, n) as j:
                    for k in range(2):
                        tile(j * 2 + (k + 2), k, False, False)
                for t in range(2 + 2 * n, NTILES):
                    tile(t, t % 2, False, t == NTILES - 1)

        with ExitStack() as ctx:
            def sb(name, shape, dt):
                return ctx.enter_context(nc.sbuf_tensor(name, shape, dt))

            NB, NR = 8, 3
            ps_c = [ctx.enter_context(nc.psum_tensor(f"ps_c{k}", [P, CH], F32)) for k in range(NR)]
            ps_y = [ctx.enter_context(nc.psum_tensor(f"ps_y{k}", [P, CH], F32)) for k in range(NR)]
            yt = [sb(f"yt{p}", [P, 2, K2, D], F32) for p in range(NB)]
            part = [sb(f"part{p}", [P, 2, D], F32) for p in range(NR)]
            moe = [sb(f"moe{p}", [P, 2, D], F32) for p in range(NR)]
            moeT = [[sb(f"moeT{p}{k}", [P, DC, 2, P], F32R) for k in "hl"] for p in range(NR)]
            res = [sb(f"res{p}", [P, 2, D], F32) for p in range(NR)]
            f32 = lambda ap: ap.bitcast(F32)
            wo_lo = sem("wo_lo")
            y_in = [sem(f"y_in{p}") for p in range(NB)]
            part_done = sem("part_done")
            moe_done = sem("moe_done")
            xb_done = sem("xb_done")
            mt_full = sem("mt_full")
            mt_hi = sem("mt_hi")
            mt_lo = sem("mt_lo")
            y_full = sem("y_full")
            res_done = sem("res_done")
            stored = [sem(f"stored{p}") for p in range(NR)]
            block = ctx.enter_context(nc.Block())

            def rows_of(dram, h):
                return dram[h * 2 * P:(h + 1) * 2 * P, :].rearrange("(t p) d -> p t d", p=P)

            @block.sync
            def _(sp):
                def load(h):
                    if h >= NB:
                        sp.wait_ge(moe_done, h - NB + 1)
                    sp.dma_start(yt[h % NB][:].rearrange("p t k d -> p t (k d)"),
                                 yk[h * 4 * P:(h + 1) * 4 * P, :].rearrange(
                                     "(t p k) d -> p t (k d)", p=P, k=K2)).then_inc(y_in[h % NB], 16)

                for h in range(NB):
                    load(h)
                for k in range(NH):
                    if k + NB < NH:
                        load(k + NB)
                    sp.wait_ge(res_done, k + 1)
                    sp.dma_start(rows_of(y_out, k), res[k % NR][:]).then_inc(stored[k % NR], 16)
                for p in range(NR):
                    sp.wait_ge(stored[p], 16 * ((NH - p + NR - 1) // NR))

            @block.gpsimd
            def _(pool):
                pool.wait_ge(wo_in, 32)
                pool.wait_ge(xall_in, 16 * (NT // XG))
                for h in range(NH):
                    xt = xall[:, 2 * h:2 * h + 2, :]
                    pool.tensor_tensor(xt, xt,
                                       bo[:].unsqueeze(1).to_broadcast([P, 2, D]), ALU.add).then_inc(xb_done, 1)

            @block.scalar
            def _(act):
                def weigh(h):
                    act.wait_ge(y_in[h % NB], 16 * (h // NB + 1))
                    if h >= NR:
                        act.wait_ge(moe_done, h - NR + 1)
                    for t in range(2):
                        last = nc.scalar.activation(part[h % NR][:, t, :], yt[h % NB][:, t, 0, :], ACT.Copy,
                                                    scale=route_w[:, 2 * h + t, 0:1])
                    last.then_inc(part_done, 1)

                weigh(0)
                weigh(1)
                for h in range(NH):
                    if h + 2 < NH:
                        weigh(h + 2)
                    act.wait_ge(mt_full, h + 1)
                    if h >= NR:
                        act.wait_ge(y_full, h - NR + 1)
                    nc.scalar.copy(moeT[h % NR][0][:].rearrange("p c t m -> p (c t m)"),
                                   ps_c[h % NR][:]).then_inc(mt_hi, 1)

            @block.tensor
            def _(pe):
                keep_warm(pe, ps_c[0], 20)
                for h in range(NH + 1):
                    if h < NH:
                        pe.wait_ge(moe_done, h + 1)
                        if h >= NR:
                            pe.wait_ge(mt_lo, h - NR + 1)
                        for c in range(DC):
                            for t in range(2):
                                at = (c * 2 + t) * P
                                last = pe.transpose(ps_c[h % NR][:, at:at + P], moe[h % NR][:, t, c * P:(c + 1) * P],
                                                    ident[:])
                        last.then_inc(mt_full, 1)
                    if h >= 1:
                        k = h - 1
                        pe.wait_ge(mt_lo, k + 1)
                        if k == 0:
                            pe.wait_ge(wo_lo, 1)
                        if k >= NR:
                            pe.wait_ge(res_done, k - NR + 1)
                        for t in range(2):
                            for c in range(DC):
                                last = mm3(pe, ps_y[k % NR][:, t * D:(t + 1) * D],
                                           [m[:, c, t, :] for m in moeT[k % NR]],
                                           [w[:, c, :] for w in wo], c == 0, c == DC - 1)
                        last.then_inc(y_full, 1)

            @block.vector
            def _(dve):
                def weigh(h):
                    b = h % NB
                    if h >= NR:
                        dve.wait_ge(mt_full, h - NR + 1)
                    dve.wait_ge(part_done, h + 1)
                    for t in range(2):
                        last = dve.scalar_tensor_tensor(moe[h % NR][:, t, :], yt[b][:, t, 1, :],
                                                        route_w[:, 2 * h + t, 1:2], part[h % NR][:, t, :],
                                                        ALU.mult, ALU.add)
                    last.then_inc(moe_done, 1)

                dve.wait_ge(wo_hi, 1)
                dve.tensor_tensor(wo[1][:], wor[:], f32(wo[0][:]), ALU.subtract).then_inc(wo_lo, 1)
                weigh(0)
                for h in range(NH + 1):
                    if h + 1 < NH:
                        weigh(h + 1)
                    if h < NH:
                        dve.wait_ge(mt_hi, h + 1)
                        dve.tensor_tensor(moeT[h % NR][1][:].rearrange("p c t m -> p (c t m)"), ps_c[h % NR][:],
                                          f32(moeT[h % NR][0][:]).rearrange("p c t m -> p (c t m)"),
                                          ALU.subtract).then_inc(mt_lo, 1)
                    if h >= 1:
                        k = h - 1
                        dve.wait_ge(y_full, k + 1)
                        dve.wait_ge(xb_done, k + 1)
                        if k >= NR:
                            dve.wait_ge(stored[k % NR], 16 * (k // NR))
                        dve.tensor_tensor(res[k % NR][:].rearrange("p t d -> p (t d)"), ps_y[k % NR][:],
                                          xall[:, 2 * k:2 * k + 2, :].rearrange("p t d -> p (t d)"),
                                          ALU.add).then_inc(res_done, 1)


_INS = ['L0_attn_x', 'L0_attn_Qw', 'L0_attn_Kw', 'L0_attn_Vw', 'L0_ffn_W_in', 'L0_ffn_b_in', 'L0_ffn_W_gate',
        'L0_ffn_b_gate', 'L0_ffn_W1', 'L0_ffn_b1', 'L0_ffn_W2', 'L0_ffn_b2', 'L0_ffn_W_out', 'L0_ffn_b_out']
_OUTS = [((1, 4096, 256), 'float32')]


def kernel(**inputs):
    import numpy as _np
    import concourse.bacc as _bacc
    from concourse import mybir as _mybir
    from concourse.bass_utils import run_bass_kernel_spmd as _run

    nc = _bacc.Bacc("TRN2", target_bir_lowering=False, num_devices=1)
    arrays, args = {}, []
    for name in _INS:
        a = _np.ascontiguousarray(inputs[name])
        arrays[f"in_{name}_dram"] = a
        args.append(nc.dram_tensor(f"in_{name}_dram", a.shape, _mybir.dt.from_np(a.dtype), kind="ExternalInput").ap())
    for i, (shape, dtype) in enumerate(_OUTS):
        dt = _mybir.dt.from_np(_np.dtype(dtype))
        args.append(nc.dram_tensor(f"out_{i}_dram", shape, dt, kind="ExternalOutput").ap())
    build_kernel(nc, *args)
    r = _run(nc, [arrays], core_ids=[0])
    got = tuple(r.results[0][f"out_{i}_dram"] for i in range(len(_OUTS)))
    return got[0]
```

```python
from contextlib import ExitStack

import concourse.bass as bass
from concourse import mybir

F32 = mybir.dt.float32
F32R = mybir.dt.float32r
BF16 = mybir.dt.bfloat16
I32 = mybir.dt.int32
U32 = mybir.dt.uint32
ALU = mybir.AluOpType
ACT = mybir.ActivationFunctionType
AX = mybir.AxisListType

P = 128
EPS = 1e-5
NEG = -3.0e38


def rows_bcast(dram, n):
    return dram.rearrange("(a n) -> a n", a=1).partition_broadcast(n).rearrange("p a n -> p (a n)")


def mm3(pe, out, w, m, start, stop):
    pe.matmul(out, w[0], m[0], start=start, stop=False)
    pe.matmul(out, w[0], m[1], start=False, stop=False)
    return pe.matmul(out, w[1], m[0], start=False, stop=stop)


def slots_of(u, NT):
    h = NT // 2 - 1
    return slice(0, 2) if u < h else slice(u - h, u - h + 1)


def make_plan(NT):
    NH = NT // 2
    nc_of = lambda i: i // 4 + 1
    plan = [("ln1", 0, 0), ("wT", 0), ("ln1", 0, 1), ("wT", 1), ("ln1", 0, 2), ("M", 0), ("xT", 0), ("Vw", 0),
            ("ln1", 1, 0), ("ln1", 1, 1), ("qm", 0), ("ln1", 1, 2), ("v", 0)]
    groups = []
    for u in range(NH + 1):
        slots = slots_of(u, NT)
        steps = [[("ln2", u, 0)], [("ln2", u, 1)], [("ln2", u, 2)], [("fT", u)],
                 [("t", u, s) for s in range(slots.start, slots.stop)],
                 [("route", u, 0)], [("route", u, 1)], [("route", u, 2), ("pre", u)],
                 [("place", u, k) for k in range(3)]]
        if u >= NH - 1:
            steps = [steps[0] + steps[1], steps[2] + steps[3], steps[4] + steps[5], steps[6] + steps[7], steps[8]]
        groups += steps
    fins, loads, last_fT = 0, 0, -1

    def ffn_group():
        nonlocal loads, last_fT
        out = []
        u = groups[0][0][1] if groups else None
        if groups and (groups[0][0][0] != "ln2" or (u < loads if u < NH - 1 else fins > NT - 2 + u - (NH - 1))):
            out = groups.pop(0)
            if out[0][0] == "fT":
                last_fT = out[0][1]
        if loads < NH - 1 and 2 * loads + 1 < fins and loads - 1 <= last_fT:
            out = out + [("ld2", loads)]
            loads += 1
        return out

    late = [("Wi", 0), ("wT", 2), ("G", 0)]
    next_b, last_pv, finished = 0, None, []
    s = 0
    while next_b < NT or groups or finished:
        scores = [("qk", s, c) for c in range(nc_of(s))] if s < NT else []
        exps = []
        if 1 <= s <= NT:
            plan.append(("mx", s - 1))
            exps = [("ex", s - 1, c) for c in range(nc_of(s - 1))]
            plan += exps[:2]
            exps = exps[2:]
        if scores:
            plan.append(scores.pop(0))
        if last_pv:
            plan.append(last_pv)
            last_pv = None
        plan += [("fin", i) for i in finished]
        fins += len(finished)
        ahead = []
        k = s // 2 + 1
        if k < NH:
            ahead = [("xT", k)] if s % 2 == 0 else [("qm", k), ("v", k)]
        if k + 1 < NH:
            if s % 2 == 0:
                ahead = ahead + [("ln1", k + 1, 0)]
            else:
                ahead = [("ln1", k + 1, 1), ahead[0], ("ln1", k + 1, 2), ahead[1]]
        last_b = min(s - (2 if s < 12 else 1), NT - 1)
        slots = [(j, c) for j in range(next_b, last_b + 1) for c in range(nc_of(j))]
        finished = list(range(next_b, last_b + 1))
        next_b = max(next_b, last_b + 1)
        placed = 0
        for n, (j, c) in enumerate(slots):
            if scores:
                plan.append(scores.pop(0))
            plan.append(("tp", j, c))
            if exps:
                plan.append(exps.pop(0))
            upto = (n + 1) * len(ahead) // len(slots)
            plan += ahead[placed:upto]
            if last_pv:
                plan.append(last_pv)
            last_pv = ("pv", j, c)
            plan += ffn_group()
            placed = upto
        plan += ahead[placed:] + scores + exps
        if not slots:
            plan += ffn_group()
        plan += late[:1]
        late = late[1:]
        s += 1
    return plan


def build_kernel(nc, x_in, Qw, Kw, Vw, W_in, b_in, W_gate, b_gate, W1, b1, W2, b2, W_out, b_out, out):
    S, D = x_in.shape[1], x_in.shape[2]
    E, F = W1.shape[0], W1.shape[2]
    K2 = 2
    NT = S // P
    NH = NT // 2
    DC = D // P
    CH = 4 * P
    NCH = S // CH
    HC = F // P
    TS = 2 * P
    REGION = S + TS
    NTILES = (K2 * S + E * (TS - 1)) // TS
    ROW = D + 1
    NOWHERE = 1.0e6
    SCALE = 1.0 / float(D) ** 0.5
    NS = 10
    GW = D + E
    assert D == 256 and E == 8 and F == 1024 and S % CH == 0

    x = x_in.rearrange("a s d -> (a s) d")
    y_out = out.rearrange("a s d -> (a s) d")
    xs = nc.dram_tensor("routed_rows", [E * REGION + TS, ROW], F32).ap()
    yk = nc.dram_tensor("expert_rows", [K2 * S, D], F32).ap()
    x2d = nc.dram_tensor("x_after_attention", [S, D], F32).ap()

    plan = make_plan(NT)
    chunk0 = [0]
    for i in range(NT):
        chunk0.append(chunk0[-1] + i // 4 + 1)
    KINDS = ("wT", "M", "G", "xT", "qm", "v", "fT", "t", "pre")
    HILO = ("M", "xT", "qm", "v", "fT")
    job, hijob = {}, {}
    for it in plan:
        if it[0] in KINDS:
            job[it] = len(job)
            if it[0] in HILO:
                hijob[it] = len(hijob)

    def tiles_of(u):
        at, h = slots_of(u, NT), min(u, NH - 1)
        return slice(2 * h + at.start, 2 * h + at.stop)

    def width(i, c):
        w = CH if c < i // 4 else (i % 4 + 1) * P
        return w, max(w, 2 * P)

    with ExitStack() as keep:
        def sbk(name, shape, dt):
            return keep.enter_context(nc.sbuf_tensor(name, shape, dt))

        def sem(name):
            return keep.enter_context(nc.semaphore(name))

        earlier = sbk("earlier", [P, E, E], F32)
        base_i = sbk("base_i", [P, E], I32)
        base = sbk("base", [P, E], F32)
        base255 = sbk("base255", [P, E], F32)
        tau_i = sbk("tau_i", [P, NTILES], I32)
        tau = sbk("tau", [P, NTILES], F32)
        cnt = sbk("cnt", [P, E], F32)
        tabi = sbk("tabi", [1, E], I32)
        vchain = sem("vchain")
        tables = sem("tables")
        chained = [0]

        def link(dve, ins):
            chained[0] += 1
            ins.then_inc(vchain, 1)
            dve.wait_ge(vchain, chained[0])

        ident = sbk("ident", [P, P], F32)
        route_w = sbk("route_w", [P, NT, K2], F32)
        tile_row = sbk("tile_row", [1, NTILES], I32)
        tile_expert = sbk("tile_expert", [1, NTILES], I32)
        pad_row = sbk("pad_row", [1, E], I32)
        scores = sbk("scores", [P, NS, CH], F32)
        assert DC * F == HC * D == 4 * CH and NS >= 10
        w1r0 = scores[:, NS - 4:NS, :].rearrange("p s n -> p (s n)").rearrange("p (c n) -> p c n", c=DC)
        w2r0 = scores[:, NS - 8:NS - 4, :].rearrange("p s n -> p (s n)").rearrange("p (c n) -> p c n", c=HC)
        in_w1 = [sem(f"in_w1{p}") for p in range(2)]
        in_w2 = [sem(f"in_w2{p}") for p in range(2)]

        def keep_warm(pe, bank, n):
            for _ in range(n):
                pe.matmul(bank[:, 0:P], ident[:], ident[:], start=True, stop=True)

        with ExitStack() as ctx:
            def sb(name, shape, dt):
                return ctx.enter_context(nc.sbuf_tensor(name, shape, dt))

            ps_s = [ctx.enter_context(nc.psum_tensor(f"ps_s{k}", [P, CH], F32)) for k in range(2)]
            ps_t = [ctx.enter_context(nc.psum_tensor(f"ps_t{k}", [P, CH], F32)) for k in range(2)]
            ps_o = [ctx.enter_context(nc.psum_tensor(f"ps_o{k}", [P, CH], F32)) for k in range(2)]
            ps_m = [ctx.enter_context(nc.psum_tensor(f"ps_m{k}", [P, CH], F32)) for k in range(2)]

            xT = [sb(f"xT{k}", [P, DC, S], F32R) for k in "hl"]
            V = [sb(f"V{k}", [P, NT, D], F32R) for k in "hl"]
            QT = [[sb(f"QT{p}{k}", [P, DC, 2 * P], F32R) for k in "hl"] for p in range(2)]
            PT = [[sb(f"PT{p}{k}", [P, CH], F32R) for k in "hl"] for p in range(2)]
            xn = [sb(f"xn{p}", [P, 2, D], F32) for p in range(2)]
            xres = [sb(f"xres{p}", [P, D], F32) for p in range(2)]
            x2 = [sb(f"x2{p}", [P, D], F32) for p in range(2)]
            xn2 = sb("xn2", [P, 2, D], F32)
            x2T = [sb(f"x2T{k}", [P, DC, 2 * P], F32R) for k in "hl"]
            trow = sb("trow", [P, 2, K2, ROW], F32)
            Mw = [sb(f"Mw{k}", [P, DC, D], F32R) for k in "hl"]
            Vws = [sb(f"Vw{k}", [P, DC, D], F32R) for k in "hl"]
            Wi = [sb(f"Wi{k}", [P, DC, GW], F32R) for k in "hl"]
            pad = sb("pad", [P, ROW], F32)
            causal = sb("causal", [P, CH], F32)
            bin_row = sb("bin_row", [P, D], F32)
            bin_col = sb("bin_col", [P, DC], F32)
            wg = sb("wg", [P, DC, E], F32)
            gate_bias = sb("gate_bias", [P, E], F32)
            bgate = sb("bgate", [P, E], F32)
            before = sb("before", [P, P], BF16)
            ones = sb("ones", [P, P], BF16)
            target_i = sb("target_i", [P, NT, K2], I32)
            target = sb("target", [P, NT, K2], F32)
            mxs = sb("mxs", [P, NT, NCH], F32)
            negm = sb("negm", [P, NT], F32)
            lsum = sb("lsum", [P, NT, NCH], F32)
            rden = sb("rden", [P, 2], F32)
            stats = [sb(f"stats{k}", [P, 2, 6], F32) for k in range(2)]
            mv = [sb(f"mv{k}", [P, 2, 2], F32) for k in range(2)]
            nw = [sb(f"nw{k}", [P, 4, 2], F32) for k in range(2)]
            lg = sb("lg", [P, 2, E], F32)
            cmp = sb("cmp", [P, 2, 2, E, E], F32)
            rank = sb("rank", [P, 2, E], F32)
            pick = [sb(f"pick{k}", [P, 2, E], F32) for k in range(K2)]
            prod = sb("prod", [P, K2, 2, E], F32)
            lk = sb("lk", [P, K2, 2], F32)
            gd = sb("gd", [P, 2], F32)
            ge = sb("ge", [P, 2], F32)
            gs = sb("gs", [P, 2], F32)
            gr = sb("gr", [P, 2], F32)
            sel = sb("sel", [P, 2, E], BF16)
            pos = sb("pos", [P, 2, E], F32)
            posf = sb("posf", [P, 2, K2], F32)
            slot = sb("slot", [P, NT, K2], U32)
            tabe = sb("tabe", [1, 4, E], F32)
            tabj = sb("tabj", [1, E, E], F32)
            f32 = lambda ap: ap.bitcast(F32)

            def unit_cols(ap, at):
                return ap[:, :, at.start * P:at.stop * P]

            wraw = [scores[:, NS - 1 - k, :].rearrange("p (c n) -> p c n", c=DC) for k in (3, 2, 0, 4)]
            wTr = [scores[:, NS - 1 - k, :].rearrange("p (c n) -> p c n", c=DC) for k in (5, 6, 1)]

            bin_wide = scores[:, NS - 3, 0:DC * P].rearrange("p (c n) -> p c n", c=DC)
            flat = scores[0:1, :, :].rearrange("p s n -> p (s n)")
            oneh = flat[:, 0:2 * NTILES * E].rearrange("p (k t e) -> p k t e", k=2, e=E)
            tabf = flat[:, 2 * NTILES * E:2 * NTILES * E + 4 * NTILES].rearrange("p (k t) -> p k t", k=4)
            assert 2 * NTILES * E + 4 * NTILES <= (NS - 8) * CH
            w_in = sem("w_in")
            qk_w_in = sem("qk_w_in")
            v_w_in = sem("v_w_in")
            x_ld = [sem(f"x_ld{p}") for p in range(2)]
            res_ld = [sem(f"res_ld{p}") for p in range(2)]
            consts = sem("consts")
            pchain = sem("pchain")
            var_ready = [sem(f"var_ready{k}") for k in (1, 2)]
            log_done = [sem(f"log_done{k}") for k in (1, 2)]
            rstd_guess = [sem(f"rstd_guess{k}") for k in (1, 2)]
            ln_done = sem("ln_done")
            ln2_done = sem("ln2_done")
            wcast = sem("wcast")
            wdone = sem("wdone")
            vw_lo = sem("vw_lo")
            misc_full = sem("misc_full")
            misc_hi = sem("misc_hi")
            misc_done = sem("misc_done")
            scores_full = sem("scores_full")
            scores_out = sem("scores_out")
            max_ready = sem("max_ready")
            exp_done = sem("exp_done")
            pt_full = sem("pt_full")
            pt_hi = sem("pt_hi")
            pt_lo = sem("pt_lo")
            pv_done = sem("pv_done")
            fin_done = sem("fin_done")
            x2_stored = [sem(f"x2_stored{p}") for p in range(2)]
            x2_ld = sem("x2_ld")
            gate_diff = sem("gate_diff")
            gate_exp = sem("gate_exp")
            sel_ready = sem("sel_ready")
            slots_ready = sem("slots_ready")
            t_ready = sem("t_ready")
            scattered = sem("scattered")
            counted = sem("counted")
            padded = sem("padded")
            block = ctx.enter_context(nc.Block())

            N_W = 6
            W1_FREE = 1 + max(c for c in range(NCH) if (chunk0[NT - 1] + c) % NS >= NS - 4)

            @block.sync
            def _(sp):
                def load_x(h):
                    sp.dma_start(xn[h % 2][:], x[h * 2 * P:(h + 1) * 2 * P, :].rearrange(
                        "(t p) d -> p t d", p=P)).then_inc(x_ld[h % 2], 16)

                load_x(0)
                for k, w, arrived in ((0, Qw, qk_w_in), (1, Kw, qk_w_in), (3, Vw, v_w_in), (2, W_in, w_in)):
                    sp.dma_start(wraw[k], w.rearrange("(c p) n -> p c n", p=P)).then_inc(arrived, 16)
                sp.dma_start(wg[:], W_gate.rearrange("(c p) n -> p c n", p=P)).then_inc(w_in, 16)
                sp.dma_start(bin_row[:], rows_bcast(b_in, P)).then_inc(w_in, 16)
                sp.dma_start(bgate[:], rows_bcast(b_gate, P)).then_inc(w_in, 16)
                for c in range(DC):
                    sp.dma_start(bin_col[:, c:c + 1],
                                 b_in[c * P:(c + 1) * P].rearrange("(p a) -> p a", a=1)).then_inc(w_in, 16)
                load_x(1)
                for it in plan:
                    if it[0] == "xT" and it[1] + 2 < NH:
                        sp.wait_ge(misc_full, job[it] + 1)
                        load_x(it[1] + 2)
                    elif it[0] == "mx":
                        i = it[1]
                        if i >= 2:
                            sp.wait_ge(fin_done, i - 1)
                        sp.dma_start(xres[i % 2][:], x[i * P:(i + 1) * P, :]).then_inc(res_ld[i % 2], 16)
                    elif it[0] == "fin":
                        i = it[1]
                        sp.wait_ge(fin_done, i + 1)
                        sp.dma_start(x2d[i * P:(i + 1) * P, :], x2[i % 2][:]).then_inc(x2_stored[i % 2], 16)
                    elif it == ("tp", NT - 1, W1_FREE):
                        sp.wait_ge(pt_full, chunk0[NT - 1] + W1_FREE)
                        sp.dma_start(w1r0, W1[0].rearrange("(c p) n -> p c n", p=P)).then_inc(in_w1[0], 16)
                    elif it == ("place", NH - 1, 0):
                        sp.wait_ge(counted, 1)
                        for e in range(E):
                            r = sp.snap(sp.value_load(pad_row[0:1, e:e + 1], min_val=0,
                                                      max_val=E * REGION - TS - P))
                            sp.dma_start(xs[bass.ds(r, TS + P), :].rearrange("(p a) d -> p a d", p=P),
                                         pad[:].unsqueeze(1).to_broadcast([P, TS // P + 1, ROW])).then_inc(padded, 16)
                        sp.dma_start(xs[E * REGION:E * REGION + TS, :].rearrange("(p a) d -> p a d", p=P),
                                     pad[:].unsqueeze(1).to_broadcast([P, TS // P, ROW])).then_inc(padded, 16)
                    elif it[0] == "ld2":
                        h = it[1]
                        for p in range(2):
                            sp.wait_ge(x2_stored[p], 16 * (h + 1))
                        if h >= 1:
                            sp.wait_ge(misc_full, job[("fT", h - 1)] + 1)
                        sp.dma_start(xn2[:], x2d[h * 2 * P:(h + 1) * 2 * P, :].rearrange(
                            "(t p) d -> p t d", p=P)).then_inc(x2_ld, 16)
                sp.wait_ge(pt_full, chunk0[NT])
                sp.dma_start(w2r0, W2[0].rearrange("(p c) n -> p c n", c=HC)).then_inc(in_w2[0], 16)
                for p in range(2):
                    sp.wait_ge(x2_stored[p], 16 * NH)
                sp.wait_ge(padded, 16 * (E + 1))

            @block.gpsimd
            def _(pool):
                done = [0]

                def link(ins):
                    done[0] += 1
                    ins.then_inc(pchain, 1)
                    pool.wait_ge(pchain, done[0])

                link(pool.memset(ident[:], 0.0))
                pool.affine_select(out=ident[:], in_=ident[:], compare_op=ALU.not_equal, fill=1.0, base=0,
                                   pattern=[[-1, P]], channel_multiplier=1).then_inc(consts, 1)
                link(pool.memset(causal[:], 0.0))
                pool.affine_select(out=causal[:, CH - P:], in_=causal[:, CH - P:], compare_op=ALU.is_ge, fill=NEG,
                                   base=0, pattern=[[-1, P]], channel_multiplier=1).then_inc(consts, 1)
                link(pool.memset(before[:], 0.0))
                pool.affine_select(out=before[:], in_=before[:], compare_op=ALU.is_ge, fill=1.0, base=0,
                                   pattern=[[-1, P]], channel_multiplier=1).then_inc(consts, 1)
                pool.memset(ones[:], 1.0).then_inc(consts, 1)
                link(pool.memset(earlier[:], 0.0))
                pool.affine_select(out=earlier[:], in_=earlier[:], compare_op=ALU.is_ge, fill=1.0, base=0,
                                   pattern=[[-1, E], [1, E]], channel_multiplier=0).then_inc(consts, 1)
                pool.iota(target_i[:], pattern=[[2 * P, NT], [1, K2]], base=0,
                          channel_multiplier=2).then_inc(consts, 1)
                pool.iota(base_i[:], pattern=[[REGION, E]], base=0, channel_multiplier=0).then_inc(consts, 1)
                pool.iota(tau_i[:], pattern=[[1, NTILES]], base=0, channel_multiplier=0).then_inc(consts, 1)
                link(pool.memset(pad[:], 0.0))
                pool.memset(pad[:, D:ROW], NOWHERE).then_inc(consts, 1)
                for it in plan:
                    if it[0] == "route" and it[2] == 0:
                        u = it[1]
                        at, tiles = slots_of(u, NT), tiles_of(u)
                        pool.wait_ge(misc_done, job[("t", u, at.stop - 1)] + 1)
                        for s in range(at.start, at.stop):
                            pool.tensor_copy(trow[:, s, 1, 0:D], trow[:, s, 0, 0:D]).then_inc(t_ready, 1)
                        pool.wait_ge(wdone, 1)
                        pool.tensor_copy(trow[:, at, :, D], target[:, tiles, :]).then_inc(t_ready, 1)
                    elif it[0] == "place" and it[2] == 1:
                        u = it[1]
                        at, tiles = slots_of(u, NT), tiles_of(u)
                        pool.wait_ge(slots_ready, u + 1)
                        if u == NH:
                            pool.wait_ge(padded, 16 * (E + 1))
                        pool.wait_ge(t_ready, tiles.stop + u + 1)
                        for s in range(at.start, at.stop):
                            for k in range(K2):
                                pool.indirect_dma_start(
                                    xs, bass.IndirectOffsetOnAxis(ap=slot[:, tiles.start + s - at.start, k:k + 1],
                                                                  axis=0),
                                    trow[:, s, k, :], None, bounds_check=E * REGION - 1).then_inc(scattered, 16)
                pool.wait_ge(scattered, 16 * K2 * NT)

            @block.scalar
            def _(act):
                act.preload_act_table_set("natural_log_exp_and_others")

                def hi(it, dst):
                    act.wait_ge(misc_full, job[it] + 1)
                    w = dst.free_size()
                    src = ps_m[job[it] % 2][:, 0:w]
                    if len(dst.shape) == 3:
                        src = src.rearrange("p (c n) -> p c n", c=dst.shape[1])
                    nc.scalar.copy(dst, src).then_inc(misc_hi, 1)

                for it in plan:
                    if it[0] == "Vw":
                        act.wait_ge(v_w_in, 16)
                        nc.scalar.copy(Vws[0][:], wraw[3]).then_inc(wcast, 1)
                    elif it[0] == "Wi":
                        act.wait_ge(w_in, 16 * N_W)
                        nc.scalar.copy(Wi[0][:, :, 0:D], wraw[2]).then_inc(wcast, 1)
                    elif it[0] == "M":
                        hi(it, Mw[0][:])
                    elif it[0] == "xT":
                        hi(it, xT[0][:, :, it[1] * 2 * P:(it[1] + 1) * 2 * P])
                    elif it[0] == "qm":
                        hi(it, QT[it[1] % 2][0][:])
                    elif it[0] == "v":
                        hi(it, V[0][:, 2 * it[1]:2 * it[1] + 2, :])
                    elif it[0] == "fT":
                        at = slots_of(it[1], NT)
                        act.wait_ge(misc_full, job[it] + 1)
                        nc.scalar.copy(unit_cols(x2T[0][:], at),
                                       unit_cols(ps_m[job[it] % 2][:].rearrange("p (c n) -> p c n", c=DC), at))\
                          .then_inc(misc_hi, 1)
                    elif it[0] == "ex":
                        _, i, c = it
                        g = chunk0[i] + c
                        w, _w = width(i, c)
                        act.wait_ge(max_ready, i + 1)
                        p = scores[:, g % NS, 0:w]
                        nc.scalar.activation(p, p, ACT.Exp, bias=negm[:, i:i + 1], scale=SCALE,
                                             accum_out=lsum[:, i, c:c + 1]).then_inc(exp_done, 1)
                    elif it[0] == "tp":
                        _, i, c = it
                        g = chunk0[i] + c
                        w, _w = width(i, c)
                        act.wait_ge(pt_full, g + 1)
                        if g >= 2:
                            act.wait_ge(pv_done, g - 1)
                        nc.scalar.copy(PT[g % 2][0][:, 0:w], ps_t[g % 2][:, 0:w]).then_inc(pt_hi, 1)
                    elif it[0] in ("ln1", "ln2") and it[2] == 1:
                        k = int(it[0] == "ln2")
                        act.wait_ge(var_ready[k], it[1] + 1)
                        at = slots_of(it[1], NT) if k else slice(0, 2)
                        nc.scalar.activation(nw[k][:, 1, at], nw[k][:, 0, at], ACT.Ln).then_inc(log_done[k], 1)
                        act.wait_ge(log_done[k], it[1] + 1)
                        nc.scalar.activation(nw[k][:, 2, at], nw[k][:, 1, at], ACT.Exp,
                                             scale=-0.5).then_inc(rstd_guess[k], 1)
                    elif it[0] == "route" and it[2] == 2:
                        act.wait_ge(gate_diff, it[1] + 1)
                        at = slots_of(it[1], NT)
                        nc.scalar.activation(ge[:, at], gd[:, at], ACT.Exp).then_inc(gate_exp, 1)

            @block.tensor
            def _(pe):
                def bank(it):
                    n = job[it]
                    if n >= 2:
                        pe.wait_ge(misc_done, n - 1)
                    return ps_m[n % 2]

                pe.wait_ge(consts, 1)
                keep_warm(pe, ps_o[0], 10)
                pe.wait_ge(consts, 9)
                for it in plan:
                    kind = it[0]
                    if kind == "wT":
                        if it[1] == 0:
                            pe.wait_ge(qk_w_in, 16 * 2)
                        elif it[1] == 2:
                            pe.wait_ge(w_in, 16 * N_W)
                        ps = bank(it)
                        for ce in range(DC):
                            for cd in range(DC):
                                at = ce * D + cd * P
                                last = pe.transpose(ps[:, at:at + P], wraw[it[1]][:, cd, ce * P:(ce + 1) * P],
                                                    ident[:])
                        last.then_inc(misc_full, 1)
                    elif kind == "M":
                        keep_warm(pe, ps_o[0], 4)
                        pe.wait_ge(misc_done, job[("wT", 1)] + 1)
                        ps = bank(it)
                        for cd in range(DC):
                            for ce in range(DC):
                                last = pe.matmul(ps[:, cd * D:(cd + 1) * D], wTr[0][:, ce, cd * P:(cd + 1) * P],
                                                 wTr[1][:, ce, :], start=(ce == 0), stop=(ce == DC - 1))
                        last.then_inc(misc_full, 1)
                    elif kind == "G":
                        pe.wait_ge(misc_done, job[("wT", 2)] + 1)
                        ps = bank(it)
                        pe.wait_ge(wdone, 3)
                        for cd in range(DC + 1):
                            for ce in range(DC):
                                w = wTr[2][:, ce, cd * P:(cd + 1) * P] if cd < DC else bin_wide[:, ce, :]
                                last = pe.matmul(ps[:, cd * E:(cd + 1) * E], w, wg[:, ce, :],
                                                 start=(ce == 0), stop=(ce == DC - 1))
                        last.then_inc(misc_full, 1)
                    elif kind in ("xT", "fT"):
                        h = it[1]
                        if kind == "xT":
                            pe.wait_ge(ln_done, h + 1)
                        else:
                            pe.wait_ge(ln2_done, h + 1)
                        src = xn[h % 2] if kind == "xT" else xn2
                        ps = bank(it)
                        slots = slots_of(h, NT) if kind == "fT" else slice(0, 2)
                        for s in range(slots.start, slots.stop):
                            for c in range(DC):
                                at = c * 2 * P + s * P
                                last = pe.transpose(ps[:, at:at + P], src[:, s, c * P:(c + 1) * P], ident[:])
                        last.then_inc(misc_full, 1)
                    elif kind == "qm":
                        h = it[1]
                        pe.wait_ge(misc_done, max(job[("xT", h)], job[("M", 0)]) + 1)
                        ps = bank(it)
                        for c2 in range(DC):
                            for c1 in range(DC):
                                last = mm3(pe, ps[:, c2 * D:(c2 + 1) * D],
                                           [m[:, c1, c2 * P:(c2 + 1) * P] for m in Mw],
                                           [t[:, c1, h * 2 * P:(h + 1) * 2 * P] for t in xT],
                                           c1 == 0, c1 == DC - 1)
                        last.then_inc(misc_full, 1)
                    elif kind == "v":
                        h = it[1]
                        pe.wait_ge(vw_lo, 1)
                        ps = bank(it)
                        for s in range(2):
                            for c in range(DC):
                                at = (2 * h + s) * P
                                last = mm3(pe, ps[:, s * D:(s + 1) * D], [t[:, c, at:at + P] for t in xT],
                                           [w[:, c, :] for w in Vws], c == 0, c == DC - 1)
                        last.then_inc(misc_full, 1)
                    elif kind == "t":
                        _, h, s = it
                        pe.wait_ge(misc_done, job[("fT", h)] + 1)
                        pe.wait_ge(wdone, 5)
                        ps = bank(it)
                        for c in range(DC):
                            last = mm3(pe, ps[:, 0:GW], [t[:, c, s * P:(s + 1) * P] for t in x2T],
                                       [w[:, c, :] for w in Wi], c == 0, c == DC - 1)
                        last.then_inc(misc_full, 1)
                    elif kind == "pre":
                        h = it[1]
                        pe.wait_ge(sel_ready, h + 1)
                        ps = bank(it)
                        at = slots_of(h, NT)
                        cols = slice(at.start * E, at.stop * E)
                        s2 = sel[:].rearrange("p t e -> p (t e)")[:, cols]
                        pe.matmul(ps[:, cols], before[:], s2, start=True, stop=True)
                        pe.matmul(ps[:, 2 * E + at.start * E:2 * E + at.stop * E], ones[:], s2,
                                  start=True, stop=True).then_inc(misc_full, 1)
                    elif kind == "qk":
                        _, i, c = it
                        g = chunk0[i] + c
                        w, wide = width(i, c)
                        if c == 0:
                            pe.wait_ge(misc_done, job[("qm", i // 2)] + 1)
                        if g >= 2:
                            pe.wait_ge(scores_out, g - 1)
                        at = (i % 2) * P
                        for d in range(DC):
                            last = mm3(pe, ps_s[g % 2][:, 0:wide], [q[:, d, at:at + P] for q in QT[i // 2 % 2]],
                                       [t[:, d, c * CH:c * CH + wide] for t in xT], d == 0, d == DC - 1)
                        last.then_inc(scores_full, 1)
                    elif kind == "tp":
                        _, i, c = it
                        g = chunk0[i] + c
                        w, _w = width(i, c)
                        pe.wait_ge(exp_done, g + 1)
                        if g >= 2:
                            pe.wait_ge(pt_lo, g - 1)
                        for k in range(w // P):
                            last = pe.transpose(ps_t[g % 2][:, k * P:(k + 1) * P],
                                                scores[:, g % NS, k * P:(k + 1) * P], ident[:])
                        last.then_inc(pt_full, 1)
                    elif kind == "pv":
                        _, i, c = it
                        g = chunk0[i] + c
                        w, _w = width(i, c)
                        pe.wait_ge(pt_lo, g + 1)
                        if c == 0:
                            pe.wait_ge(misc_done, job[("v", i // 2)] + 1)
                            if i >= 2:
                                pe.wait_ge(fin_done, i - 1)
                        for k in range(w // P):
                            kt = c * 4 + k
                            last = mm3(pe, ps_o[i % 2][:, 0:D], [p[:, k * P:(k + 1) * P] for p in PT[g % 2]],
                                       [v[:, kt, :] for v in V], kt == 0, kt == i)
                        last.then_inc(pv_done, 1)
                keep_warm(pe, ps_o[0], 22)

            @block.vector
            def _(dve):
                def layernorm(k, n, src, dst, ready, piece, at=slice(0, 2)):
                    v, _log, y, a = (nw[k][:, j, at] for j in range(4))
                    slots = range(at.start, at.stop)
                    if piece == 0:
                        for s in slots:
                            last = dve.bn_stats(stats[k][:, s, :], src[s])
                        link(dve, last)
                        for s in slots:
                            last = dve.bn_aggr(mv[k][:, s, :], stats[k][:, s, :])
                        link(dve, last)
                        dve.tensor_scalar(v, mv[k][:, at, 1], EPS, None, ALU.add).then_inc(var_ready[k], 1)
                    elif piece == 2:
                        dve.wait_ge(rstd_guess[k], n + 1)
                        link(dve, dve.scalar_tensor_tensor(a, y, -0.5, y, ALU.mult, ALU.mult))
                        link(dve, dve.tensor_tensor(a, a, v, ALU.mult))
                        link(dve, dve.scalar_tensor_tensor(y, a, 1.5, y, ALU.add, ALU.mult))
                        for s in slots:
                            last = dve.tensor_scalar(dst[:, s, :], src[s], mv[k][:, s, 0:1], nw[k][:, 2, s:s + 1],
                                                     ALU.subtract, ALU.mult)
                        last.then_inc(ready, 1)

                def lo(it, dst, hi_part):
                    dve.wait_ge(misc_hi, hijob[it] + 1)
                    src = ps_m[job[it] % 2][:, 0:dst.free_size()].rearrange("p (c n) -> p c n", c=dst.shape[1])
                    dve.tensor_tensor(dst, src, f32(hi_part), ALU.subtract).then_inc(misc_done, 1)

                dve.wait_ge(consts, 9)
                dve.tensor_copy(target[:], target_i[:]).then_inc(wdone, 1)
                dve.tensor_copy(tau[:], tau_i[:])
                dve.tensor_scalar(base255[:], base_i[:], -float(TS - 1), None, ALU.add)
                dve.tensor_copy(base[:], base_i[:]).then_inc(wdone, 1)
                dve.wait_ge(wdone, 2)
                link(dve, dve.tensor_copy(cnt[:], base[:]))
                for it in plan:
                    kind = it[0]
                    if kind == "Vw":
                        dve.wait_ge(wcast, 1)
                        dve.tensor_tensor(Vws[1][:], wraw[3], f32(Vws[0][:]), ALU.subtract).then_inc(vw_lo, 1)
                    elif kind == "Wi":
                        dve.wait_ge(w_in, 16 * N_W)
                        for c in range(DC):
                            last = dve.tensor_copy(bin_wide[:, c, :], bin_col[:, c:c + 1].to_broadcast([P, P]))
                        last.then_inc(wdone, 1)
                        dve.wait_ge(wcast, 2)
                        dve.tensor_tensor(Wi[1][:, :, 0:D], wraw[2], f32(Wi[0][:, :, 0:D]),
                                          ALU.subtract).then_inc(wdone, 1)
                    elif kind == "wT":
                        dve.wait_ge(misc_full, job[it] + 1)
                        dve.tensor_copy(wTr[it[1]], ps_m[job[it] % 2][:].rearrange("p (c n) -> p c n", c=DC))\
                           .then_inc(misc_done, 1)
                    elif kind == "M":
                        lo(it, Mw[1][:], Mw[0][:])
                    elif kind == "G":
                        dve.wait_ge(misc_full, job[it] + 1)
                        ps = ps_m[job[it] % 2]
                        g2 = ps[:, 0:DC * E].rearrange("p (c e) -> p c e", c=DC)
                        link(dve, dve.tensor_copy(Wi[0][:, :, D:GW], g2))
                        dve.tensor_tensor(Wi[1][:, :, D:GW], g2, f32(Wi[0][:, :, D:GW]),
                                          ALU.subtract).then_inc(wdone, 1)
                        dve.tensor_tensor(gate_bias[:], ps[:, DC * E:(DC + 1) * E], bgate[:],
                                          ALU.add).then_inc(misc_done, 1)
                        dve.wait_ge(misc_done, job[it] + 1)
                    elif kind == "ln1":
                        h = it[1]
                        dve.wait_ge(x_ld[h % 2], 16 * (h // 2 + 1))
                        layernorm(0, h, [xn[h % 2][:, s, :] for s in range(2)], xn[h % 2], ln_done, it[2])
                    elif kind == "ln2":
                        u = it[1]
                        if u < NH - 1:
                            dve.wait_ge(x2_ld, 16 * (u + 1))
                            layernorm(1, u, [xn2[:, s, :] for s in range(2)], xn2, ln2_done, it[2])
                        else:
                            if it[2] == 0:
                                dve.wait_ge(fin_done, NT - 1 + u - (NH - 1))
                            elif it[2] == 2:
                                dve.wait_ge(misc_full, job[("fT", NH - 2)] + 1)
                            layernorm(1, u, [x2[s][:] for s in range(2)], xn2, ln2_done, it[2], slots_of(u, NT))
                    elif kind == "xT":
                        at = slice(it[1] * 2 * P, (it[1] + 1) * 2 * P)
                        lo(it, xT[1][:, :, at], xT[0][:, :, at])
                    elif kind == "qm":
                        q = QT[it[1] % 2]
                        lo(it, q[1][:], q[0][:])
                    elif kind == "v":
                        at = slice(2 * it[1], 2 * it[1] + 2)
                        lo(it, V[1][:, at, :], V[0][:, at, :])
                    elif kind == "fT":
                        at = slots_of(it[1], NT)
                        dve.wait_ge(misc_hi, hijob[it] + 1)
                        dve.tensor_tensor(unit_cols(x2T[1][:], at),
                                          unit_cols(ps_m[job[it] % 2][:].rearrange("p (c n) -> p c n", c=DC), at),
                                          f32(unit_cols(x2T[0][:], at)), ALU.subtract).then_inc(misc_done, 1)
                    elif kind == "qk":
                        _, i, c = it
                        g = chunk0[i] + c
                        w, _w = width(i, c)
                        dve.wait_ge(scores_full, g + 1)
                        if g >= NS:
                            dve.wait_ge(pt_full, g - NS + 1)
                        diag = c == i // 4
                        mask = causal[:, CH - w:] if diag else causal[:, 0:1].to_broadcast([P, w])
                        dve.tensor_tensor_reduce(scores[:, g % NS, 0:w], ps_s[g % 2][:, 0:w], mask, 1.0, NEG,
                                                 ALU.add, ALU.max, mxs[:, i, c:c + 1]).then_inc(scores_out, 1)
                    elif kind == "mx":
                        i = it[1]
                        dve.wait_ge(scores_out, chunk0[i + 1])
                        link(dve, dve.tensor_reduce(negm[:, i:i + 1], mxs[:, i, 0:i // 4 + 1], AX.X, ALU.max))
                        dve.tensor_scalar(negm[:, i:i + 1], negm[:, i:i + 1], -SCALE, None,
                                          ALU.mult).then_inc(max_ready, 1)
                    elif kind == "tp":
                        _, i, c = it
                        g = chunk0[i] + c
                        w, _w = width(i, c)
                        dve.wait_ge(pt_hi, g + 1)
                        dve.tensor_tensor(PT[g % 2][1][:, 0:w], ps_t[g % 2][:, 0:w],
                                          f32(PT[g % 2][0][:, 0:w]), ALU.subtract).then_inc(pt_lo, 1)
                    elif kind == "fin":
                        i = it[1]
                        dve.wait_ge(pv_done, chunk0[i + 1])
                        link(dve, dve.tensor_reduce(rden[:, 0:1], lsum[:, i, 0:i // 4 + 1], AX.X, ALU.add))
                        link(dve, dve.reciprocal(rden[:, 1:2], rden[:, 0:1]))
                        dve.wait_ge(res_ld[i % 2], 16 * (i // 2 + 1))
                        if i >= 2:
                            dve.wait_ge(x2_stored[i % 2], 16 * (i // 2))
                        dve.scalar_tensor_tensor(x2[i % 2][:], ps_o[i % 2][:, 0:D], rden[:, 1:2],
                                                 xres[i % 2][:], ALU.mult, ALU.add).then_inc(fin_done, 1)
                    elif kind == "t":
                        _, h, s = it
                        if s == 0 and h >= 1:
                            dve.wait_ge(scattered, 16 * K2 * tiles_of(h - 1).stop)
                        dve.wait_ge(misc_full, job[it] + 1)
                        ps = ps_m[job[it] % 2]
                        dve.tensor_tensor(trow[:, s, 0, 0:D], ps[:, 0:D], bin_row[:], ALU.add)
                        dve.tensor_tensor(lg[:, s, :], ps[:, D:GW], gate_bias[:], ALU.add)\
                           .then_inc(misc_done, 1)
                    elif kind == "route" and it[2] == 0:
                        at = slots_of(it[1], NT)
                        sh = [P, at.stop - at.start, E, E]
                        dve.wait_ge(misc_done, job[("t", it[1], at.stop - 1)] + 1)
                        lj = lg[:, at].unsqueeze(2).to_broadcast(sh)
                        le = lg[:, at].unsqueeze(3).to_broadcast(sh)
                        gt, eq = cmp[:, 0, at], cmp[:, 1, at]
                        link(dve, dve.tensor_tensor(eq, lj, le, ALU.is_equal))
                        dve.tensor_tensor(gt, lj, le, ALU.is_gt)
                        link(dve, dve.tensor_tensor(eq, eq, earlier[:].unsqueeze(1).to_broadcast(sh), ALU.mult))
                        link(dve, dve.tensor_tensor(gt, gt, eq, ALU.add))
                    elif kind == "route" and it[2] == 1:
                        at = slots_of(it[1], NT)
                        link(dve, dve.tensor_reduce(rank[:, at], cmp[:, 0, at], AX.X, ALU.add))
                        dve.tensor_scalar(sel[:, at], rank[:, at], float(K2), None, ALU.is_lt).then_inc(sel_ready, 1)
                        for k in range(K2):
                            last = dve.tensor_scalar(pick[k][:, at], rank[:, at], float(k), None, ALU.is_equal)
                        link(dve, last)
                    elif kind == "route":
                        at = slots_of(it[1], NT)
                        for k in range(K2):
                            last = dve.tensor_tensor(prod[:, k, at], pick[k][:, at], lg[:, at], ALU.mult)
                        link(dve, last)
                        link(dve, dve.tensor_reduce(lk[:, :, at], prod[:, :, at], AX.X, ALU.add))
                        dve.tensor_tensor(gd[:, at], lk[:, 1, at], lk[:, 0, at], ALU.subtract).then_inc(gate_diff, 1)
                    elif kind == "pre":
                        dve.wait_ge(misc_full, job[it] + 1)
                        ps = ps_m[job[it] % 2]
                        at = slots_of(it[1], NT)
                        for s in range(at.start, at.stop):
                            dve.tensor_tensor(pos[:, s, :], ps[:, s * E:(s + 1) * E], cnt[:], ALU.add)
                            last = dve.tensor_tensor(cnt[:], ps[:, (2 + s) * E:(3 + s) * E], cnt[:], ALU.add)
                            if s < at.stop - 1:
                                link(dve, last)
                        last.then_inc(misc_done, 1)
                        dve.wait_ge(misc_done, job[it] + 1)
                        if it[1] == NH - 1:
                            dve.tensor_copy(pad_row[:], cnt[0:1, :]).then_inc(counted, 1)
                    elif kind == "place" and it[2] == 0:
                        at = slots_of(it[1], NT)
                        for k in range(K2):
                            last = dve.tensor_tensor(prod[:, k, at], pick[k][:, at], pos[:, at], ALU.mult)
                        link(dve, last)
                    elif kind == "place" and it[2] == 1:
                        at = slots_of(it[1], NT)
                        for k in range(K2):
                            last = dve.tensor_reduce(posf[:, at, k], prod[:, k, at], AX.X, ALU.add)
                        link(dve, last)
                        dve.tensor_copy(slot[:, tiles_of(it[1]), :], posf[:, at]).then_inc(slots_ready, 1)
                    elif kind == "place":
                        u = it[1]
                        at, tiles = slots_of(u, NT), tiles_of(u)
                        dve.wait_ge(gate_exp, u + 1)
                        link(dve, dve.tensor_scalar(gs[:, at], ge[:, at], 1.0, None, ALU.add))
                        link(dve, dve.reciprocal(gr[:, at], gs[:, at]))
                        dve.tensor_copy(route_w[:, tiles, 0], gr[:, at])
                        link(dve, dve.tensor_tensor(route_w[:, tiles, 1], gr[:, at], ge[:, at], ALU.mult))

                rowf, expf, part = (tabf[:, k, :] for k in range(3))
                tiles, excl, incl, delta = (tabe[:, k, :] for k in range(4))
                t0 = tau[0:1, :]
                link(dve, dve.tensor_tensor(tabi[:], cnt[0:1, :], base255[0:1, :], ALU.subtract))
                link(dve, dve.tensor_scalar(tabi[:], tabi[:], TS.bit_length() - 1, None, ALU.logical_shift_right))
                link(dve, dve.tensor_scalar(tiles, tabi[:], 1.0, None, ALU.max))
                link(dve, dve.tensor_tensor(tabj[:], earlier[0:1], tiles.unsqueeze(1).to_broadcast([1, E, E]),
                                            ALU.mult))
                link(dve, dve.tensor_reduce(excl, tabj[:], AX.X, ALU.add))
                dve.tensor_tensor(incl, excl, tiles, ALU.add)
                link(dve, dve.scalar_tensor_tensor(delta, excl, -float(TS), base[0:1, :], ALU.mult, ALU.add))
                sh = [1, NTILES, E]
                tb = t0.unsqueeze(2).to_broadcast(sh)
                dve.tensor_tensor(oneh[:, 1], tb, excl.unsqueeze(1).to_broadcast(sh), ALU.is_ge)
                link(dve, dve.tensor_tensor(oneh[:, 0], tb, incl.unsqueeze(1).to_broadcast(sh), ALU.is_ge))
                dve.tensor_reduce(expf, oneh[:, 0], AX.X, ALU.add)
                link(dve, dve.tensor_tensor(oneh[:, 1], oneh[:, 1], oneh[:, 0], ALU.subtract))
                link(dve, dve.tensor_tensor(oneh[:, 1], oneh[:, 1], delta.unsqueeze(1).to_broadcast(sh), ALU.mult))
                dve.tensor_scalar(tile_expert[:], expf, float(E - 1), None, ALU.min)
                link(dve, dve.tensor_reduce(rowf, oneh[:, 1], AX.X, ALU.add))
                link(dve, dve.scalar_tensor_tensor(rowf, t0, float(TS), rowf, ALU.mult, ALU.add))
                link(dve, dve.scalar_tensor_tensor(part, oneh[:, 0, :, E - 1], float(E * REGION), rowf,
                                                   ALU.mult, ALU.add))
                dve.tensor_scalar(tile_row[:], part, float(E * REGION), None, ALU.min).then_inc(tables, 1)
                dve.wait_ge(tables, 1)

        XG = 8
        xall = sbk("xall", [P, NT, D], F32)
        wor = sbk("wor", [P, DC, D], F32)
        wo = [sbk(f"wo{k}", [P, DC, D], F32R) for k in "hl"]
        bo = sbk("bo", [P, D], F32)
        wo_in = sem("wo_in")
        wo_hi = sem("wo_hi")
        xall_in = sem("xall_in")

        with ExitStack() as ctx:
            def sb(name, shape, dt):
                return ctx.enter_context(nc.sbuf_tensor(name, shape, dt))

            ps_x = ctx.enter_context(nc.psum_tensor("ps_x", [P, CH], F32))
            NHB = 3
            ps_h = [ctx.enter_context(nc.psum_tensor(f"ps_h{k}", [P, CH], F32)) for k in range(NHB)]
            ps_e = [[ctx.enter_context(nc.psum_tensor(f"ps_e{p}{s}", [P, CH], F32)) for s in range(2)]
                    for p in range(2)]
            HQ = HC // 2
            xr = [sb(f"xr{p}", [P, 2, ROW], F32) for p in range(2)]
            w1r = [w1r0, sb("w1r1", [P, DC, F], F32)[:]]
            w2r = [w2r0, sb("w2r1", [P, HC, D], F32)[:]]
            b1s = [sb(f"b1s{p}", [P, HC], F32) for p in range(2)]
            b2s = [sb(f"b2s{p}", [P, D], F32) for p in range(2)]
            w1 = [[sb(f"w1{p}{k}", [P, DC, HC, P], F32R) for k in "hl"] for p in range(2)]
            w2 = [[sb(f"w2{p}{k}", [P, HC, D], F32R) for k in "hl"] for p in range(2)]
            xrT = [sb(f"xrT{k}", [P, DC, TS], F32R) for k in "hl"]
            mid = sb("mid", [P, HC, TS], F32)
            midT = [sb(f"midT{k}", [P, HC, TS], F32R) for k in "hl"]
            esb = [sb(f"esb{p}", [P, 2, D], F32) for p in range(2)]
            eidx = [sb(f"eidx{p}", [P, 2], U32) for p in range(2)]
            f32 = lambda ap: ap.bitcast(F32)

            in_x = [sem(f"in_x{p}") for p in range(2)]
            in_b = [sem(f"in_b{p}") for p in range(2)]
            xt_full = sem("xt_full")
            xt_hi = sem("xt_hi")
            xt_lo = sem("xt_lo")
            w1_hi = sem("w1_hi")
            w1_lo = sem("w1_lo")
            w2_hi = sem("w2_hi")
            w2_lo = sem("w2_lo")
            hid_full = sem("hid_full")
            relu_done = sem("relu_done")
            mid_hi = sem("mid_hi")
            mid_lo = sem("mid_lo")
            h1_done = sem("h1_done")
            e_full = sem("e_full")
            e_out = sem("e_out")
            idx_done = sem("idx_done")
            e_stored = [sem(f"e_stored{p}") for p in range(2)]
            block = ctx.enter_context(nc.Block())

            def over_tiles(eng, body, first):
                n = (NTILES - first) // 2
                with eng.Fori(0, n) as j:
                    for k in range(2):
                        body(j * 2 + (first + k), (first + k) % 2)
                for t in range(first + 2 * n, NTILES):
                    body(t, t % 2)

            def half(t):
                return t // 2

            @block.sync
            def _(sp):
                def load(t, p, head):
                    r = sp.snap(sp.value_load(tile_row[0:1, bass.ds(t, 1)], min_val=0, max_val=E * REGION))
                    e = sp.snap(sp.value_load(tile_expert[0:1, bass.ds(t, 1)], min_val=0, max_val=E - 1))
                    if not head:
                        done = sp.snap(t - 1)
                        q1 = sp.snap(DC * (t - 1))
                        q2 = sp.snap(HQ * (t - 1))
                        sp.wait_ge(xt_full, done)
                        sp.wait_ge(idx_done, done)
                    sp.dma_start(xr[p][:], xs[bass.ds(r, TS), :].rearrange("(a q) d -> q a d", q=P))\
                      .then_inc(in_x[p], 16)
                    if not head:
                        sp.wait_ge(w1_lo, q1)
                    sp.dma_start(w1r[p], W1[bass.ds(e, 1), :, :].rearrange("a (c q) n -> q (a c) n", q=P))\
                      .then_inc(in_w1[p], 16)
                    if not head:
                        sp.wait_ge(w2_lo, q2)
                    sp.dma_start(w2r[p], W2[bass.ds(e, 1), :, :].rearrange("a (q c) n -> q (a c) n", c=HC))\
                      .then_inc(in_w2[p], 16)
                    if not head:
                        sp.wait_ge(e_out, done)
                    sp.dma_start(b1s[p][:], b1[bass.ds(e, 1), :].rearrange("a (q c) -> q (a c)", c=HC))\
                      .then_inc(in_b[p], 16)
                    sp.dma_start(b2s[p][:], b2[bass.ds(e, 1), :].partition_broadcast(P).rearrange(
                        "q a n -> q (a n)")).then_inc(in_b[p], 16)

                sp.dma_start(xr[0][:], xs[0:TS, :].rearrange("(a q) d -> q a d", q=P)).then_inc(in_x[0], 16)
                sp.dma_start(b1s[0][:], b1[0].rearrange("(q c) -> q c", c=HC)).then_inc(in_b[0], 16)
                sp.dma_start(b2s[0][:], rows_bcast(b2[0], P)).then_inc(in_b[0], 16)
                load(1, 1, True)
                over_tiles(sp, lambda t, p: load(t, p, False), 2)
                sp.dma_start(wor[:], W_out.rearrange("(c p) n -> p c n", p=P)).then_inc(wo_in, 16)
                sp.dma_start(bo[:], rows_bcast(b_out, P)).then_inc(wo_in, 16)
                for g in range(NT // XG):
                    sp.dma_start(xall[:, g * XG:(g + 1) * XG, :], x2d[g * XG * P:(g + 1) * XG * P, :].rearrange(
                        "(t p) d -> p t d", p=P)).then_inc(xall_in, 16)

            @block.gpsimd
            def _(pool):
                def store(t, p, head):
                    if not head:
                        pool.wait_ge(e_stored[p], 32 * half(t))
                    pool.wait_ge(in_x[p], 16 * (half(t) + 1))
                    pool.tensor_copy(eidx[p][:], xr[p][:, :, D]).then_inc(idx_done, 1)
                    pool.wait_ge(idx_done, t + 1)
                    pool.wait_ge(e_out, t + 1)
                    for s in range(2):
                        pool.indirect_dma_start(
                            yk, bass.IndirectOffsetOnAxis(ap=eidx[p][:, s:s + 1], axis=0), esb[p][:, s, :], None,
                            bounds_check=K2 * S - 1, oob_is_err=False).then_inc(e_stored[p], 16)

                for t in range(NTILES):
                    store(t, t % 2, t < 2)
                for p in range(2):
                    pool.wait_ge(e_stored[p], 32 * ((NTILES - p + 1) // 2))

            @block.scalar
            def _(act):
                def split_w1(t, p, c):
                    if c == 0:
                        act.wait_ge(in_w1[p], 16 * (half(t) + 1))
                    nc.scalar.copy(w1[p][0][:, c].rearrange("q h m -> q m h"),
                                   w1r[p][:, c, :].rearrange("q (m h) -> q m h", h=HC)).then_inc(w1_hi, 1)

                def split_w2(t, p, q):
                    if q == 0:
                        act.wait_ge(in_w2[p], 16 * (half(t) + 1))
                    nc.scalar.copy(w2[p][0][:, 2 * q:2 * q + 2, :], w2r[p][:, 2 * q:2 * q + 2, :]).then_inc(w2_hi, 1)

                def rows_hi(t):
                    act.wait_ge(xt_full, t + 1)
                    nc.scalar.copy(xrT[0][:], ps_x[:].rearrange("q (c n) -> q c n", c=DC)).then_inc(xt_hi, 1)

                def tile(t, p, last):
                    for q in range(HQ):
                        if q == 0:
                            act.wait_ge(in_b[p], 32 * (half(t) + 1))
                        act.wait_ge(hid_full, t * HQ + (q + 1))
                        for k in range(2):
                            h = 2 * q + k
                            r = nc.scalar.activation(mid[:, h, :], ps_h[q % 2][:, k * TS:(k + 1) * TS], ACT.Relu,
                                                     bias=b1s[p][:, h:h + 1])
                        r.then_inc(relu_done, 1)
                        if not last and q < DC:
                            split_w1(t + 1, 1 - p, q)
                    if not last:
                        rows_hi(t + 1)
                        for q in range(HQ):
                            split_w2(t + 1, 1 - p, q)

                for c in range(DC):
                    split_w1(0, 0, c)
                rows_hi(0)
                for q in range(HQ):
                    split_w2(0, 0, q)
                n = (NTILES - 1) // 2
                with act.Fori(0, n) as j:
                    for k in range(2):
                        tile(j * 2 + k, k, False)
                for t in range(2 * n, NTILES):
                    tile(t, t % 2, t == NTILES - 1)
                act.wait_ge(wo_in, 32)
                nc.scalar.copy(wo[0][:], wor[:]).then_inc(wo_hi, 1)

            @block.tensor
            def _(pe):
                def rows(t, p, head):
                    if not head:
                        pe.wait_ge(xt_lo, t)
                    pe.wait_ge(in_x[p], 16 * (half(t) + 1))
                    for s in range(2):
                        for c in range(DC):
                            at = c * TS + s * P
                            last = pe.transpose(ps_x[:, at:at + P], xr[p][:, s, c * P:(c + 1) * P], ident[:])
                    last.then_inc(xt_full, 1)

                def tile(t, p, first, head, last_tile):
                    for q in range(HQ):
                        if not first:
                            pe.wait_ge(relu_done, t * HQ + (q - 1))
                        elif q >= 2:
                            pe.wait_ge(relu_done, q - 1)
                        if q == 0:
                            pe.wait_ge(xt_lo, t + 1)
                            pe.wait_ge(w1_lo, DC * (t + 1))
                        for k in range(2):
                            h = 2 * q + k
                            for c in range(DC):
                                last = mm3(pe, ps_h[q % 2][:, k * TS:(k + 1) * TS], [w[:, c, h, :] for w in w1[p]],
                                           [x_[:, c, :] for x_ in xrT], c == 0, c == DC - 1)
                        last.then_inc(hid_full, 1)
                    if not last_tile:
                        rows(t + 1, 1 - p, False)
                    for q in range(HQ):
                        pe.wait_ge(mid_lo, t * HQ + (q + 1))
                        if q == 0:
                            pe.wait_ge(w2_lo, HQ * (t + 1))
                            if not head:
                                pe.wait_ge(e_out, t - 1)
                        for h in (2 * q, 2 * q + 1):
                            for s in range(2):
                                last = mm3(pe, ps_e[p][s][:, 0:D], [m[:, h, s * P:(s + 1) * P] for m in midT],
                                           [w[:, h, :] for w in w2[p]], h == 0, h == HC - 1)
                    last.then_inc(e_full, 1)

                keep_warm(pe, ps_e[0][0], 12)
                rows(0, 0, True)
                tile(0, 0, True, True, False)
                tile(1, 1, False, True, False)
                n = (NTILES - 3) // 2
                with pe.Fori(0, n) as j:
                    for k in range(2):
                        tile(j * 2 + (k + 2), k, False, False, False)
                for t in range(2 + 2 * n, NTILES):
                    tile(t, t % 2, False, False, t == NTILES - 1)
                keep_warm(pe, ps_x, 16)

            @block.vector
            def _(dve):
                def split_w1(t, p, c):
                    dve.wait_ge(w1_hi, DC * t + (c + 1))
                    dve.tensor_tensor(w1[p][1][:, c].rearrange("q h m -> q m h"),
                                      w1r[p][:, c, :].rearrange("q (m h) -> q m h", h=HC),
                                      f32(w1[p][0][:, c]).rearrange("q h m -> q m h"),
                                      ALU.subtract).then_inc(w1_lo, 1)

                def split_w2(t, p, q):
                    dve.wait_ge(w2_hi, HQ * t + (q + 1))
                    at = slice(2 * q, 2 * q + 2)
                    dve.tensor_tensor(w2[p][1][:, at, :], w2r[p][:, at, :], f32(w2[p][0][:, at, :]),
                                      ALU.subtract).then_inc(w2_lo, 1)

                def rows_lo(t):
                    dve.wait_ge(xt_hi, t + 1)
                    dve.tensor_tensor(xrT[1][:], ps_x[:].rearrange("q (c n) -> q c n", c=DC), f32(xrT[0][:]),
                                      ALU.subtract).then_inc(xt_lo, 1)

                def tile(t, p, head, last):
                    for q in range(HQ):
                        at = slice(2 * q, 2 * q + 2)
                        dve.wait_ge(relu_done, t * HQ + (q + 1))
                        dve.tensor_copy(midT[0][:, at, :], mid[:, at, :]).then_inc(mid_hi, 1)
                        dve.wait_ge(mid_hi, t * HQ + (q + 1))
                        dve.tensor_tensor(midT[1][:, at, :], mid[:, at, :], f32(midT[0][:, at, :]),
                                          ALU.subtract).then_inc(mid_lo, 1)
                        if not last and q < DC:
                            split_w1(t + 1, 1 - p, q)
                    if not last:
                        rows_lo(t + 1)
                        for q in range(HQ):
                            split_w2(t + 1, 1 - p, q)
                    if not head:
                        dve.wait_ge(e_stored[p], 32 * half(t))
                    dve.wait_ge(e_full, t + 1)
                    for s in range(2):
                        r = dve.tensor_tensor(esb[p][:, s, :], ps_e[p][s][:, 0:D], b2s[p][:], ALU.add)
                    r.then_inc(e_out, 1)

                for c in range(DC):
                    split_w1(0, 0, c)
                rows_lo(0)
                for q in range(HQ):
                    split_w2(0, 0, q)
                tile(0, 0, True, False)
                tile(1, 1, True, False)
                n = (NTILES - 3) // 2
                with dve.Fori(0, n) as j:
                    for k in range(2):
                        tile(j * 2 + (k + 2), k, False, False)
                for t in range(2 + 2 * n, NTILES):
                    tile(t, t % 2, False, t == NTILES - 1)

        with ExitStack() as ctx:
            def sb(name, shape, dt):
                return ctx.enter_context(nc.sbuf_tensor(name, shape, dt))

            NB, NR = 8, 4
            ps_c = [ctx.enter_context(nc.psum_tensor(f"ps_c{k}", [P, CH], F32)) for k in range(NR)]
            ps_y = [ctx.enter_context(nc.psum_tensor(f"ps_y{k}", [P, CH], F32)) for k in range(NR)]
            yt = [sb(f"yt{p}", [P, 2, K2, D], F32) for p in range(NB)]
            part = [sb(f"part{p}", [P, 2, D], F32) for p in range(NR)]
            moe = [sb(f"moe{p}", [P, 2, D], F32) for p in range(NR)]
            moeT = [[sb(f"moeT{p}{k}", [P, DC, 2, P], F32R) for k in "hl"] for p in range(NR)]
            res = [sb(f"res{p}", [P, 2, D], F32) for p in range(NR)]
            f32 = lambda ap: ap.bitcast(F32)
            wo_lo = sem("wo_lo")
            y_in = [sem(f"y_in{p}") for p in range(NB)]
            part_done = sem("part_done")
            moe_done = sem("moe_done")
            xb_done = sem("xb_done")
            mt_full = sem("mt_full")
            mt_hi = sem("mt_hi")
            mt_lo = sem("mt_lo")
            y_full = sem("y_full")
            res_done = sem("res_done")
            stored = [sem(f"stored{p}") for p in range(NR)]
            block = ctx.enter_context(nc.Block())

            def rows_of(dram, h):
                return dram[h * 2 * P:(h + 1) * 2 * P, :].rearrange("(t p) d -> p t d", p=P)

            @block.sync
            def _(sp):
                def load(h):
                    if h >= NB:
                        sp.wait_ge(moe_done, h - NB + 1)
                    sp.dma_start(yt[h % NB][:].rearrange("p t k d -> p t (k d)"),
                                 yk[h * 4 * P:(h + 1) * 4 * P, :].rearrange(
                                     "(t p k) d -> p t (k d)", p=P, k=K2)).then_inc(y_in[h % NB], 16)

                for h in range(NB):
                    load(h)
                for k in range(NH):
                    if k + NB < NH:
                        load(k + NB)
                    sp.wait_ge(res_done, k + 1)
                    sp.dma_start(rows_of(y_out, k), res[k % NR][:]).then_inc(stored[k % NR], 16)
                for p in range(NR):
                    sp.wait_ge(stored[p], 16 * ((NH - p + NR - 1) // NR))

            @block.gpsimd
            def _(pool):
                pool.wait_ge(wo_in, 32)
                pool.wait_ge(xall_in, 16 * (NT // XG))
                for h in range(NH):
                    xt = xall[:, 2 * h:2 * h + 2, :]
                    pool.tensor_tensor(xt, xt,
                                       bo[:].unsqueeze(1).to_broadcast([P, 2, D]), ALU.add).then_inc(xb_done, 1)

            @block.scalar
            def _(act):
                def weigh(h):
                    act.wait_ge(y_in[h % NB], 16 * (h // NB + 1))
                    if h >= NR:
                        act.wait_ge(moe_done, h - NR + 1)
                    for t in range(2):
                        last = nc.scalar.activation(part[h % NR][:, t, :], yt[h % NB][:, t, 0, :], ACT.Copy,
                                                    scale=route_w[:, 2 * h + t, 0:1])
                    last.then_inc(part_done, 1)

                weigh(0)
                weigh(1)
                for h in range(NH):
                    if h + 2 < NH:
                        weigh(h + 2)
                    act.wait_ge(mt_full, h + 1)
                    if h >= NR:
                        act.wait_ge(y_full, h - NR + 1)
                    nc.scalar.copy(moeT[h % NR][0][:].rearrange("p c t m -> p (c t m)"),
                                   ps_c[h % NR][:]).then_inc(mt_hi, 1)

            @block.tensor
            def _(pe):
                keep_warm(pe, ps_c[0], 20)
                for h in range(NH + 1):
                    if h < NH:
                        pe.wait_ge(moe_done, h + 1)
                        if h >= NR:
                            pe.wait_ge(mt_lo, h - NR + 1)
                        for c in range(DC):
                            for t in range(2):
                                at = (c * 2 + t) * P
                                last = pe.transpose(ps_c[h % NR][:, at:at + P], moe[h % NR][:, t, c * P:(c + 1) * P],
                                                    ident[:])
                        last.then_inc(mt_full, 1)
                    if h >= 1:
                        k = h - 1
                        pe.wait_ge(mt_lo, k + 1)
                        if k == 0:
                            pe.wait_ge(wo_lo, 1)
                        if k >= NR:
                            pe.wait_ge(res_done, k - NR + 1)
                        for t in range(2):
                            for c in range(DC):
                                last = mm3(pe, ps_y[k % NR][:, t * D:(t + 1) * D],
                                           [m[:, c, t, :] for m in moeT[k % NR]],
                                           [w[:, c, :] for w in wo], c == 0, c == DC - 1)
                        last.then_inc(y_full, 1)

            @block.vector
            def _(dve):
                def weigh(h):
                    b = h % NB
                    if h >= NR:
                        dve.wait_ge(mt_full, h - NR + 1)
                    dve.wait_ge(part_done, h + 1)
                    for t in range(2):
                        last = dve.scalar_tensor_tensor(moe[h % NR][:, t, :], yt[b][:, t, 1, :],
                                                        route_w[:, 2 * h + t, 1:2], part[h % NR][:, t, :],
                                                        ALU.mult, ALU.add)
                    last.then_inc(moe_done, 1)

                dve.wait_ge(wo_hi, 1)
                dve.tensor_tensor(wo[1][:], wor[:], f32(wo[0][:]), ALU.subtract).then_inc(wo_lo, 1)
                weigh(0)
                for h in range(NH + 1):
                    if h + 1 < NH:
                        weigh(h + 1)
                    if h < NH:
                        dve.wait_ge(mt_hi, h + 1)
                        dve.tensor_tensor(moeT[h % NR][1][:].rearrange("p c t m -> p (c t m)"), ps_c[h % NR][:],
                                          f32(moeT[h % NR][0][:]).rearrange("p c t m -> p (c t m)"),
                                          ALU.subtract).then_inc(mt_lo, 1)
                    if h >= 1:
                        k = h - 1
                        dve.wait_ge(y_full, k + 1)
                        dve.wait_ge(xb_done, k + 1)
                        if k >= NR:
                            dve.wait_ge(stored[k % NR], 16 * (k // NR))
                        dve.tensor_tensor(res[k % NR][:].rearrange("p t d -> p (t d)"), ps_y[k % NR][:],
                                          xall[:, 2 * k:2 * k + 2, :].rearrange("p t d -> p (t d)"),
                                          ALU.add).then_inc(res_done, 1)


_INS = ['L0_attn_x', 'L0_attn_Qw', 'L0_attn_Kw', 'L0_attn_Vw', 'L0_ffn_W_in', 'L0_ffn_b_in', 'L0_ffn_W_gate',
        'L0_ffn_b_gate', 'L0_ffn_W1', 'L0_ffn_b1', 'L0_ffn_W2', 'L0_ffn_b2', 'L0_ffn_W_out', 'L0_ffn_b_out']
_OUTS = [((1, 4096, 256), 'float32')]


def kernel(**inputs):
    import numpy as _np
    import concourse.bacc as _bacc
    from concourse import mybir as _mybir
    from concourse.bass_utils import run_bass_kernel_spmd as _run

    nc = _bacc.Bacc("TRN2", target_bir_lowering=False, num_devices=1)
    arrays, args = {}, []
    for name in _INS:
        a = _np.ascontiguousarray(inputs[name])
        arrays[f"in_{name}_dram"] = a
        args.append(nc.dram_tensor(f"in_{name}_dram", a.shape, _mybir.dt.from_np(a.dtype), kind="ExternalInput").ap())
    for i, (shape, dtype) in enumerate(_OUTS):
        dt = _mybir.dt.from_np(_np.dtype(dtype))
        args.append(nc.dram_tensor(f"out_{i}_dram", shape, dt, kind="ExternalOutput").ap())
    build_kernel(nc, *args)
    r = _run(nc, [arrays], core_ids=[0])
    got = tuple(r.results[0][f"out_{i}_dram"] for i in range(len(_OUTS)))
    return got[0]
```
